# Optimizing a Trainium2 kernel written in Bass

```python
import numpy as np
import jax
import jax.numpy as jnp

def _softmax(x, axis=-1):
    return jax.nn.softmax(x, axis=axis)

def _gelu(x):
    return jax.nn.gelu(x, approximate=True)

def _silu(x):
    return jax.nn.silu(x)

def _sigmoid(x):
    return jax.nn.sigmoid(x)

def _layernorm(x, axis=-1, eps=1e-05):
    m = jnp.mean(x, axis=axis, keepdims=True)
    v = jnp.var(x, axis=axis, keepdims=True)
    return (x - m) / jnp.sqrt(v + eps)

def _scatter_add(tgt, idx, src, axis=0):
    return tgt.at[idx].add(src)

def _segment_sum(src, seg, n):
    return jax.ops.segment_sum(src, seg, n)
kernel_name = 'mk_decoder_preln_d1_seqx_r8_9b11ec'

def setup_inputs(seed: int=0):
    np.random.seed(seed)
    _w = jnp.asarray

    def _rec_inputs():
        import jax
        import jax.numpy as jnp
        _rk = jax.random.key(seed)
        x = -0.0002928 + 1 * jax.random.normal(jax.random.fold_in(_rk, 1), (64, 64, 128), jnp.float32)
        _lenS = 64 - jax.random.randint(jax.random.fold_in(_rk, 7), (64,), 0, max(1, 64 // 4) + 1, jnp.int32)
        _lenS2 = 64 - jax.random.randint(jax.random.fold_in(_rk, 8), (64,), 0, max(1, 64 // 4) + 1, jnp.int32)
        _ctx_1024P = jax.random.normal(jax.random.fold_in(_rk, 11), (64, 16, 128), jnp.float32)
        _ctx_1024c = jax.random.dirichlet(jax.random.fold_in(_rk, 511), 0.3 * jnp.ones((16,), jnp.float32), (64, 64))
        _ctx_1024t = jnp.einsum('bsk,bkd->bsd', _ctx_1024c, _ctx_1024P)
        _ctx_1024t = _ctx_1024t * jax.lax.rsqrt(jnp.mean(jnp.square(_ctx_1024t)) + 1e-12) * 0.953939
        ctx_1024 = -1.39393e-06 + 0.999914 * (_ctx_1024t + 0.3 * jax.random.normal(jax.random.fold_in(_rk, 611), (64, 64, 128), jnp.float32))
        return (x, ctx_1024)
    x, ctx_1024 = _rec_inputs()

    def _L0_attn_setup():
        import jax, jax.numpy as jnp
        import numpy as np
        import math
        DIM = 128
        NUM_HEADS = 16
        HEAD_DIM = DIM // NUM_HEADS
        MAX_BIAS = 8.0
        SCALE = HEAD_DIM ** (-0.5)

        def _alibi_slopes(n):

            def pow2(n):
                start = 2.0 ** (-2.0 ** (-(math.log2(n) - 3)))
                return [start * start ** i for i in range(n)]
            if math.log2(n).is_integer():
                return pow2(n)
            c = 2 ** math.floor(math.log2(n))
            return pow2(c) + _alibi_slopes(2 * c)[0::2][:n - c]

        def _rotate_half(t):
            t1, t2 = jnp.split(t, 2, axis=-1)
            return jnp.concatenate([-t2, t1], axis=-1)
        key = jax.random.key(seed)
        k1, k2, k3, k4 = jax.random.split(key, 4)
        B, N, C = (2, 256, DIM)
        x = jax.random.normal(k1, (B, N, C), dtype=jnp.float32)
        qkv_w = jax.random.normal(k2, (3 * C, C), dtype=jnp.float32) * C ** (-0.5)
        proj_w = jax.random.normal(k3, (C, C), dtype=jnp.float32) * C ** (-0.5)
        proj_b = jax.random.normal(k4, (C,), dtype=jnp.float32) * 0.01
        slopes = jnp.asarray(np.array(_alibi_slopes(NUM_HEADS), dtype=np.float32))
        return {'x': x, 'qkv_w': qkv_w, 'proj_w': proj_w, 'proj_b': proj_b, 'slopes': slopes}
    _L0_attn_all = _L0_attn_setup()
    _L0_attn_in = {k: v for k, v in _L0_attn_all.items() if k in ('qkv_w', 'proj_w', 'proj_b', 'slopes')}
    del _L0_attn_all

    def _L0_xattn_setup():
        import jax, jax.numpy as jnp
        import numpy as np
        D_MODEL = 128
        NUM_HEADS = 16
        D_K = D_MODEL // NUM_HEADS
        B, S = (2, 256)
        key = jax.random.key(seed)
        ks = jax.random.split(key, 11)
        sc = 1.0 / np.sqrt(D_MODEL)
        inp = {'query': jax.random.normal(ks[0], (B, S, D_MODEL), jnp.float32), 'key': jax.random.normal(ks[1], (B, S, D_MODEL), jnp.float32), 'value': jax.random.normal(ks[2], (B, S, D_MODEL), jnp.float32), 'Wq': jax.random.normal(ks[3], (D_MODEL, D_MODEL), jnp.float32) * sc, 'bq': jax.random.normal(ks[4], (D_MODEL,), jnp.float32) * sc, 'Wk': jax.random.normal(ks[5], (D_MODEL, D_MODEL), jnp.float32) * sc, 'bk': jax.random.normal(ks[6], (D_MODEL,), jnp.float32) * sc, 'Wv': jax.random.normal(ks[7], (D_MODEL, D_MODEL), jnp.float32) * sc, 'bv': jax.random.normal(ks[8], (D_MODEL,), jnp.float32) * sc, 'Wo': jax.random.normal(ks[9], (D_MODEL, D_MODEL), jnp.float32) * sc, 'bo': jax.random.normal(ks[10], (D_MODEL,), jnp.float32) * sc}
        return inp
    _L0_xattn_all = _L0_xattn_setup()
    _L0_xattn_in = {k: v for k, v in _L0_xattn_all.items() if k in ('Wq', 'bq', 'Wk', 'bk', 'Wv', 'bv', 'Wo', 'bo')}
    del _L0_xattn_all

    def _L0_ffn_setup():
        import jax, jax.numpy as jnp
        import numpy as np
        B, N, D, H, E = (4, 128, 128, 16, 8)
        DK = D // H
        HID = 4 * D
        EPS = 1e-05

        def _layernorm(x, w, b):
            m = jnp.mean(x, axis=-1, keepdims=True)
            v = jnp.mean(jnp.square(x - m), axis=-1, keepdims=True)
            return (x - m) * jax.lax.rsqrt(v + EPS) * w + b

        def _msa(x, w_qkv, w_proj):
            b, n, d = x.shape
            qkv = (x @ w_qkv).reshape(b, n, 3, H, DK)
            q = qkv[:, :, 0].transpose(0, 2, 1, 3)
            k = qkv[:, :, 1].transpose(0, 2, 1, 3)
            v = qkv[:, :, 2].transpose(0, 2, 1, 3)
            attn = jnp.einsum('bhnd,bhmd->bhnm', q, k) * (1.0 / np.sqrt(DK))
            attn = jax.nn.softmax(attn, axis=-1)
            y = jnp.einsum('bhnm,bhmd->bhnd', attn, v)
            y = y.transpose(0, 2, 1, 3).reshape(b, n, d)
            return y @ w_proj

        def _moe_mlp(x, gate_w, gate_b, w1, w2):
            b, n, d = x.shape
            xf = x.reshape(b * n, d)
            logits = xf @ gate_w + gate_b
            one_hot = jax.nn.one_hot(jnp.argmax(logits, axis=-1), E, dtype=xf.dtype)
            h = jax.nn.gelu(jnp.einsum('td,edh->teh', xf, w1), approximate=True)
            y = jnp.einsum('teh,ehd->ted', h, w2)
            out = jnp.einsum('te,ted->td', one_hot, y)
            return out.reshape(b, n, d)
        key = jax.random.key(seed)
        ks = jax.random.split(key, 8)
        s = 0.02
        return {'x': jax.random.normal(ks[0], (B, N, D), jnp.float32), 'ln1_w': jnp.ones((D,), jnp.float32), 'ln1_b': jnp.zeros((D,), jnp.float32), 'w_qkv': jax.random.normal(ks[1], (D, 3 * D), jnp.float32) * s, 'w_proj': jax.random.normal(ks[2], (D, D), jnp.float32) * s, 'ln2_w': jnp.ones((D,), jnp.float32), 'ln2_b': jnp.zeros((D,), jnp.float32), 'gate_w': jax.random.normal(ks[3], (D, E), jnp.float32) * s, 'gate_b': jnp.zeros((E,), jnp.float32), 'w1': jax.random.normal(ks[4], (E, D, HID), jnp.float32) * s, 'w2': jax.random.normal(ks[5], (E, HID, D), jnp.float32) * s}
    _L0_ffn_all = _L0_ffn_setup()
    _L0_ffn_in = {k: v for k, v in _L0_ffn_all.items() if k in ('ln1_w', 'ln1_b', 'w_qkv', 'w_proj', 'ln2_w', 'ln2_b', 'gate_w', 'gate_b', 'w1', 'w2')}
    del _L0_ffn_all
    return {'x': x, 'ctx_1024': ctx_1024, 'L0_attn_qkv_w': _L0_attn_in['qkv_w'], 'L0_attn_proj_w': _L0_attn_in['proj_w'], 'L0_attn_proj_b': _L0_attn_in['proj_b'], 'L0_attn_slopes': _L0_attn_in['slopes'], 'L0_xattn_Wq': _L0_xattn_in['Wq'], 'L0_xattn_bq': _L0_xattn_in['bq'], 'L0_xattn_Wk': _L0_xattn_in['Wk'], 'L0_xattn_bk': _L0_xattn_in['bk'], 'L0_xattn_Wv': _L0_xattn_in['Wv'], 'L0_xattn_bv': _L0_xattn_in['bv'], 'L0_xattn_Wo': _L0_xattn_in['Wo'], 'L0_xattn_bo': _L0_xattn_in['bo'], 'L0_ffn_ln1_w': _L0_ffn_in['ln1_w'], 'L0_ffn_ln1_b': _L0_ffn_in['ln1_b'], 'L0_ffn_w_qkv': _L0_ffn_in['w_qkv'], 'L0_ffn_w_proj': _L0_ffn_in['w_proj'], 'L0_ffn_ln2_w': _L0_ffn_in['ln2_w'], 'L0_ffn_ln2_b': _L0_ffn_in['ln2_b'], 'L0_ffn_gate_w': _L0_ffn_in['gate_w'], 'L0_ffn_gate_b': _L0_ffn_in['gate_b'], 'L0_ffn_w1': _L0_ffn_in['w1'], 'L0_ffn_w2': _L0_ffn_in['w2']}

def reference(x, ctx_1024, L0_attn_qkv_w, L0_attn_proj_w, L0_attn_proj_b, L0_attn_slopes, L0_xattn_Wq, L0_xattn_bq, L0_xattn_Wk, L0_xattn_bk, L0_xattn_Wv, L0_xattn_bv, L0_xattn_Wo, L0_xattn_bo, L0_ffn_ln1_w, L0_ffn_ln1_b, L0_ffn_w_qkv, L0_ffn_w_proj, L0_ffn_ln2_w, L0_ffn_ln2_b, L0_ffn_gate_w, L0_ffn_gate_b, L0_ffn_w1, L0_ffn_w2):
    import jax
    import jax.numpy as jnp

    def _L0_attn_ref(x, qkv_w, proj_w, proj_b, slopes):
        import jax, jax.numpy as jnp
        import numpy as np
        import math
        DIM = 128
        NUM_HEADS = 16
        HEAD_DIM = DIM // NUM_HEADS
        MAX_BIAS = 8.0
        SCALE = HEAD_DIM ** (-0.5)

        def _alibi_slopes(n):

            def pow2(n):
                start = 2.0 ** (-2.0 ** (-(math.log2(n) - 3)))
                return [start * start ** i for i in range(n)]
            if math.log2(n).is_integer():
                return pow2(n)
            c = 2 ** math.floor(math.log2(n))
            return pow2(c) + _alibi_slopes(2 * c)[0::2][:n - c]

        def _rotate_half(t):
            t1, t2 = jnp.split(t, 2, axis=-1)
            return jnp.concatenate([-t2, t1], axis=-1)
        B, N, C = x.shape
        H, D = (NUM_HEADS, HEAD_DIM)
        qkv = (x @ qkv_w.T).reshape(B, N, 3, H, D).transpose(2, 0, 3, 1, 4)
        q, k, v = (qkv[0], qkv[1], qkv[2])
        inv_freq = 1.0 / 10000.0 ** (jnp.arange(0, D, 2, dtype=jnp.float32) / D)
        freqs = jnp.arange(N, dtype=jnp.float32)[:, None] * inv_freq[None, :]
        sin = jnp.tile(jnp.sin(freqs), (1, 2))
        cos = jnp.tile(jnp.cos(freqs), (1, 2))
        q = q * cos + _rotate_half(q) * sin
        k = k * cos + _rotate_half(k) * sin
        attn = jnp.einsum('bhqd,bhkd->bhqk', q, k) * SCALE
        pos = jnp.arange(N, dtype=jnp.float32)
        diff = pos[None, :] - pos[:, None]
        diff = jnp.where(diff > 0, 0.0, diff)
        alibi = diff[None, :, :] * slopes[:, None, None] * MAX_BIAS
        attn = attn + alibi[None]
        w = jax.nn.softmax(attn, axis=-1)
        out = jnp.einsum('bhqk,bhkd->bhqd', w, v)
        out = out.transpose(0, 2, 1, 3).reshape(B, N, C)
        return out @ proj_w.T + proj_b

    def _L0_xattn_ref(query, key, value, Wq, bq, Wk, bk, Wv, bv, Wo, bo):
        import jax, jax.numpy as jnp
        import numpy as np
        D_MODEL = 128
        NUM_HEADS = 16
        D_K = D_MODEL // NUM_HEADS
        B, S = (2, 256)
        b = query.shape[0]
        Q = query @ Wq.T + bq
        K = key @ Wk.T + bk
        V = value @ Wv.T + bv
        Q = Q.reshape(b, -1, NUM_HEADS, D_K).transpose(0, 2, 1, 3)
        K = K.reshape(b, -1, NUM_HEADS, D_K).transpose(0, 2, 1, 3)
        V = V.reshape(b, -1, NUM_HEADS, D_K).transpose(0, 2, 1, 3)
        scores = jnp.einsum('bhqd,bhkd->bhqk', Q, K) / jnp.sqrt(jnp.float32(D_K))
        attn = jax.nn.softmax(scores, axis=-1)
        out = jnp.einsum('bhqk,bhkd->bhqd', attn, V)
        out = out.transpose(0, 2, 1, 3).reshape(b, -1, D_MODEL)
        return out @ Wo.T + bo

    def _L0_ffn_ref(x, ln1_w, ln1_b, w_qkv, w_proj, ln2_w, ln2_b, gate_w, gate_b, w1, w2):
        import jax, jax.numpy as jnp
        import numpy as np
        B, N, D, H, E = (4, 128, 128, 16, 8)
        DK = D // H
        HID = 4 * D
        EPS = 1e-05

        def _layernorm(x, w, b):
            m = jnp.mean(x, axis=-1, keepdims=True)
            v = jnp.mean(jnp.square(x - m), axis=-1, keepdims=True)
            return (x - m) * jax.lax.rsqrt(v + EPS) * w + b

        def _msa(x, w_qkv, w_proj):
            b, n, d = x.shape
            qkv = (x @ w_qkv).reshape(b, n, 3, H, DK)
            q = qkv[:, :, 0].transpose(0, 2, 1, 3)
            k = qkv[:, :, 1].transpose(0, 2, 1, 3)
            v = qkv[:, :, 2].transpose(0, 2, 1, 3)
            attn = jnp.einsum('bhnd,bhmd->bhnm', q, k) * (1.0 / np.sqrt(DK))
            attn = jax.nn.softmax(attn, axis=-1)
            y = jnp.einsum('bhnm,bhmd->bhnd', attn, v)
            y = y.transpose(0, 2, 1, 3).reshape(b, n, d)
            return y @ w_proj

        def _moe_mlp(x, gate_w, gate_b, w1, w2):
            b, n, d = x.shape
            xf = x.reshape(b * n, d)
            logits = xf @ gate_w + gate_b
            one_hot = jax.nn.one_hot(jnp.argmax(logits, axis=-1), E, dtype=xf.dtype)
            h = jax.nn.gelu(jnp.einsum('td,edh->teh', xf, w1), approximate=True)
            y = jnp.einsum('teh,ehd->ted', h, w2)
            out = jnp.einsum('te,ted->td', one_hot, y)
            return out.reshape(b, n, d)
        x = x + _msa(_layernorm(x, ln1_w, ln1_b), w_qkv, w_proj)
        x = x + _moe_mlp(_layernorm(x, ln2_w, ln2_b), gate_w, gate_b, w1, w2)
        return x
    x = x + _L0_attn_ref(_layernorm(x, axis=-1), L0_attn_qkv_w, L0_attn_proj_w, L0_attn_proj_b, L0_attn_slopes)
    x = x + _L0_xattn_ref(_layernorm(x, axis=-1), ctx_1024, ctx_1024, L0_xattn_Wq, L0_xattn_bq, L0_xattn_Wk, L0_xattn_bk, L0_xattn_Wv, L0_xattn_bv, L0_xattn_Wo, L0_xattn_bo)
    x = x + _L0_ffn_ref(_layernorm(x, axis=-1), L0_ffn_ln1_w, L0_ffn_ln1_b, L0_ffn_w_qkv, L0_ffn_w_proj, L0_ffn_ln2_w, L0_ffn_ln2_b, L0_ffn_gate_w, L0_ffn_gate_b, L0_ffn_w1, L0_ffn_w2)
    return x

_drawn_inputs = setup_inputs


def setup_inputs(seed=0):
    import zlib

    import numpy as np

    out = dict(_drawn_inputs(seed))
    spreads = {'L0_ffn_ln1_w': (1.0, 0.6),
     'L0_ffn_ln1_b': (0.0, 0.8),
     'L0_ffn_ln2_w': (1.0, 0.6),
     'L0_ffn_ln2_b': (0.0, 2.0),
     'L0_ffn_gate_b': (0.0, 0.353)}
    factors = {'L0_attn_proj_b': 6.099,
     'L0_xattn_bq': 2.976,
     'L0_xattn_bk': 64.0,
     'L0_ffn_w_qkv': 4.466,
     'L0_ffn_w_proj': 4.386}
    for name, (base, spread) in spreads.items():
        noise = np.random.default_rng([zlib.crc32(name.encode()), seed]).standard_normal(out[name].shape)
        drawn = base * np.exp(spread * noise) if base else spread * noise
        out[name] = jnp.asarray(drawn.astype(out[name].dtype))
    for name, factor in factors.items():
        out[name] = (out[name] * factor).astype(out[name].dtype)
    return out
```

```python
import concourse.bass as bass
from concourse import mybir
from collections import namedtuple
from contextlib import ExitStack

F32 = mybir.dt.float32
BF16 = mybir.dt.bfloat16
F16 = mybir.dt.float16
I32 = mybir.dt.int32
ALU = mybir.AluOpType
ACT = mybir.ActivationFunctionType
AX = mybir.AxisListType

P = 128
SEQS, SEQ, DIM, HEADS, HD = 64, 64, 128, 16, 8
TOKENS = SEQS * SEQ
TILES = TOKENS // P
TPU = 2
UNITS = TILES // TPU
COLS = TPU * P
LAYERS = 3
EPS = 1e-5
SCALE = HD ** -0.5
HALF = HEADS // 2
EXPERTS, HID = 8, 512
CHUNKS = HID // P
SLOT_TILES = (TOKENS - EXPERTS) // P + EXPERTS
RING = 3
GROUPS = 4
assert SLOT_TILES % RING == 0

Unit = namedtuple("Unit", "layer u n least")

CONST = {}
CONST_COLS = 0
for _name, _n in (("ident", P), ("pick", P), ("head_mask", HEADS), ("mb_mask", HEADS), ("sel0", P), ("sel1", P),
                  ("dist_qk", SEQ), ("dist_kq", SEQ), ("cos", SEQ), ("sin", SEQ), ("before", P),
                  ("first", EXPERTS), ("slot128", TILES), ("tile_no", SLOT_TILES)):
    CONST[_name] = (CONST_COLS, CONST_COLS + _n)
    CONST_COLS += _n


def decoder(nc, ins, out, slots_in, slots_out):
    with ExitStack() as ctx:
        def sb(name, shape, dt=F32):
            return ctx.enter_context(nc.sbuf_tensor(name, shape, dt))

        def sem(name):
            return ctx.enter_context(nc.semaphore(name))

        consts = sb("consts", [P, CONST_COLS])

        def const(name):
            a, b = CONST[name]
            return consts[:, a:b]

        ident = const("ident")
        x = sb("x", [P, TILES, DIM])
        y = sb("y", [P, TILES, DIM])
        z = sb("z", [P, TILES, DIM])
        ctx_in = sb("ctx_in", [P, 2, TPU, DIM])
        wqkv = sb("wqkv", [P, LAYERS, 3, DIM])
        wrot = sb("wrot", [P, 2, DIM])
        wo = sb("wo", [P, LAYERS, 2, 2, DIM])
        cols = sb("cols", [P, 6])
        rows = sb("rows", [P, 3, DIM])
        slopes = sb("slopes", [P, HEADS])
        gate_w = sb("gate_w", [P, EXPERTS])
        gate_b = sb("gate_b", [P, EXPERTS])
        w1 = sb("w1", [P, EXPERTS * HID])
        w2 = sb("w2", [P, EXPERTS * HID])
        pick16 = sb("pick16", [P, P], F16)
        pickbf = sb("pickbf", [P, SEQ], BF16)
        sel = sb("sel", [P, TPU, P], BF16)
        alibi_qk = sb("alibi_qk", [P, HEADS, SEQ], F16)
        alibi_kq = sb("alibi_kq", [P, HEADS, SEQ], F16)
        stats = sb("stats", [P, TPU, 6])
        mom = sb("mom", [P, TPU, 2])
        veps = sb("veps", [P, TPU])
        rstd = sb("rstd", [P, TPU])
        stats2 = sb("stats2", [P, TPU, 6])
        mom2 = sb("mom2", [P, TPU, 2])
        veps2 = sb("veps2", [P, TPU])
        rstd2 = sb("rstd2", [P, TPU])
        mhalf = sb("mhalf", [P, TPU])
        eps = sb("eps", [P, TPU])
        carrier = sb("carrier", [P, 1])
        xn = sb("xn", [P, TPU, DIM])
        xT = sb("xT", [P, COLS])
        cT = sb("cT", [P, COLS])
        rope_a = sb("rope_a", [P, 2 * COLS])
        rope_b = sb("rope_b", [P, 2 * COLS])
        qkT = sb("qkT", [P, 2, 2, COLS])
        qm = sb("qm", [P, 2, HEADS, COLS])
        km = sb("km", [P, 2, HEADS, COLS])
        vb = sb("vb", [P, 2, TPU, HEADS, 18])
        mrow = sb("mrow", [P, TPU, HEADS])
        mx = sb("mx", [P, TPU, 2, 2, HEADS], BF16)
        mb = sb("mb", [P, HEADS, SEQ], BF16)
        prob = sb("prob", [P, TPU, HEADS * SEQ])
        oT = sb("oT", [P, 2 * COLS])
        rc = sb("rc", [P, TPU * HALF, 2])
        on = sb("on", [P, TPU, 2, HALF, HD])
        hT = sb("hT", [P, COLS])
        delta = sb("delta", [P, TPU, DIM])
        qm_flat = qm[:, :, :, :].rearrange("p a h c -> p (a h c)")
        km_flat = km[:, :, :, :].rearrange("p a h c -> p (a h c)")
        free = [0, 0]

        def view(flat, k, shape, dt=F32):
            n = 1
            for d in shape:
                n *= d
            a = flat[:, free[k]:free[k] + n].bitcast(dt) if dt != F32 else flat[:, free[k]:free[k] + n]
            free[k] += n
            names = "abc"[:len(shape)]
            return a.rearrange(f"p ({' '.join(names)}) -> p {' '.join(names)}", **dict(zip(names, shape)))

        zn = view(qm_flat, 0, [2, TPU, DIM])
        zT = view(qm_flat, 0, [2, COLS])
        xs = view(qm_flat, 0, [RING, DIM])
        xsT = view(qm_flat, 0, [RING, P])
        hs = view(qm_flat, 0, [RING, HID])
        hsT = view(qm_flat, 0, [RING, HID])
        ys = view(qm_flat, 0, [RING, DIM])
        gstats = view(km_flat, 1, [2, TPU, 6])
        gmom = view(km_flat, 1, [2, TPU, 2])
        gveps = view(km_flat, 1, [2, TPU])
        grstd = view(km_flat, 1, [2, TPU])
        logits = view(km_flat, 1, [TILES, EXPERTS])
        best = view(km_flat, 1, [TILES])
        tie = view(km_flat, 1, [TILES, EXPERTS])
        tie_best = view(km_flat, 1, [TILES])
        count = view(km_flat, 1, [2, TILES, EXPERTS])
        filled = view(km_flat, 1, [EXPERTS, TILES])
        used = view(km_flat, 1, [EXPERTS])
        ends = view(km_flat, 1, [2, EXPERTS])
        base = view(km_flat, 1, [EXPERTS])
        place = view(km_flat, 1, [3, TILES, EXPERTS])
        slot_f = view(km_flat, 1, [TILES])
        passed = view(km_flat, 1, [SLOT_TILES, EXPERTS])
        expert_f = view(km_flat, 1, [SLOT_TILES])
        zero = sb("zero", [P, DIM])
        onehot = sb("onehot", [P, TILES, EXPERTS], BF16)
        before = sb("before", [P, P], BF16)
        ones = sb("ones", [P, P], BF16)
        slot = sb("slot", [P, TILES], I32)
        expert = sb("expert", [P, SLOT_TILES], I32)

        psum = ctx.enter_context(nc.psum_tensor("psum", [P, 8, 512], F32))
        s_ps = psum[:, 0:2, :].rearrange("p a c -> p (a c)")
        st_ps = psum[:, 2:4, :].rearrange("p a c -> p (a c)")
        pv_ps = psum[:, 4, :]
        m0 = psum[:, 5, :]
        m1 = psum[:, 6, :]
        m2 = psum[:, 7, :]

        c_in, w_in, x_in, moe_in = sem("c_in"), sem("w_in"), sem("x_in"), sem("moe_in")
        ctx_sem = [sem("ctx_in0"), sem("ctx_in1")]
        ctx_used = sem("ctx_used")
        setup = sem("setup")
        setup_pool = sem("setup_pool")
        alibi_step = sem("alibi_step")
        d_stats, d_mom, d_xn = sem("d_stats"), sem("d_mom"), sem("d_xn")
        d_stats2, d_mom2, d_y = sem("d_stats2"), sem("d_mom2"), sem("d_y")
        d_max, d_mhi, d_mx, d_mb = sem("d_max"), sem("d_mhi"), sem("d_mx"), sem("d_mb")
        d_rope, d_qk, d_qm, d_v = sem("d_rope"), sem("d_qk"), sem("d_qm"), sem("d_v")
        d_rc, d_on, d_delta, d_res = sem("d_rc"), sem("d_on"), sem("d_delta"), sem("d_res")
        p_xT, p_qk, p_rot, p_v = sem("p_xT"), sem("p_qk"), sem("p_rot"), sem("p_v")
        p_s, p_mT, p_st, p_pv = sem("p_s"), sem("p_mT"), sem("p_st"), sem("p_pv")
        p_t1, p_t2, p_out = sem("p_t1"), sem("p_t2"), sem("p_out")
        a_xT, a_qk, a_exp, a_oT, a_hT = sem("a_xT"), sem("a_qk"), sem("a_exp"), sem("a_oT"), sem("a_hT")
        g_veps, g_rstd, g_km = sem("g_veps"), sem("g_rstd"), sem("g_km")
        g_veps2, g_rstd2 = sem("g_veps2"), sem("g_rstd2")
        stored = sem("stored")
        zeroed = sem("zeroed")
        r_stats, r_mom, r_veps, r_rstd = sem("r_stats"), sem("r_mom"), sem("r_veps"), sem("r_rstd")
        r_zn, r_zT, r_zT_sb = sem("r_zn"), sem("r_zT"), sem("r_zT_sb")
        r_logits, r_biased, route, counted = sem("r_logits"), sem("r_biased"), sem("route"), sem("counted")
        routed, scattered, xy_sum = sem("routed"), sem("scattered"), sem("xy_sum")
        e_in = [sem(f"e_in{r}") for r in range(RING)]
        e_out = [sem(f"e_out{r}") for r in range(RING)]
        e_xT, e_xT_sb, e_up, e_gelu = sem("e_xT"), sem("e_xT_sb"), sem("e_up"), sem("e_gelu")
        e_hT, e_hT_sb, e_down, e_y = sem("e_hT"), sem("e_hT_sb"), sem("e_down"), sem("e_y")
        gathered = [sem(f"gathered{g}") for g in range(GROUPS)]
        summed = sem("summed")


        def unit(layer, u, least=None):
            least = u if least is None else least
            if least < 0:
                layer, u, least = layer - 1, u + UNITS, least + UNITS
            return Unit(layer, u, layer * UNITS + u, layer * UNITS + least) if 0 <= layer < LAYERS else None

        def pipeline(eng, step):
            for layer in range(LAYERS + 1):
                peeled = 4 if layer == 0 else 2
                for u in range(peeled):
                    step(unit(layer, u), unit(layer, u - 1), unit(layer, u - 2), u % 2)
                if layer < LAYERS:
                    with eng.Fori(peeled // 2, UNITS // 2) as i:
                        for par in (0, 1):
                            step(*(unit(layer, 2 * i + (par - k), peeled + par - k) for k in range(3)), par)

        def gate_pipeline(eng, step):
            for s in range(4):
                step(s, s, s % 2)
            with eng.Fori(2, UNITS // 2) as i:
                for par in (0, 1):
                    step(2 * i + par, 4 + par, par)
            for s in range(UNITS, UNITS + 3):
                step(s, s, s % 2)

        def behind(s, least, lag, end):
            if least < lag or (isinstance(s, int) and s - lag >= end):
                return None
            return s - lag

        def expert_pipeline(eng, step, lag):
            for s in range(2 * RING):
                step(s, s, s % RING, s // RING)
            with eng.Fori(2, SLOT_TILES // RING) as lap:
                for r in range(RING):
                    step(RING * lap + r, 2 * RING + r, r, lap)
            for s in range(SLOT_TILES, SLOT_TILES + lag):
                step(s, s, s % RING, s // RING)

        def tok(par_t, b):
            return slice(par_t * P + b * SEQ, par_t * P + (b + 1) * SEQ)

        block = ctx.enter_context(nc.Block())

        @block.sync
        def _(sp):
            sp.dma_start(consts[:, :], ins["consts"]).then_inc(c_in, 16)
            xv = ins["x"].rearrange("(t r) s d -> (r s) t d", r=2)
            sp.dma_start(x[:, 0:4, :], xv[:, 0:4, :]).then_inc(x_in, 16)
            for dst, name in ((wqkv[:, :, :, :].rearrange("p a b c -> p (a b c)"), "wqkv"),
                              (wrot[:, :, :].rearrange("p a c -> p (a c)"), "wrot"), (cols[:, :], "cols"),
                              (rows[:, :, :].rearrange("p a c -> p (a c)"), "rows"), (slopes[:, :], "slopes"),
                              (gate_w[:, :], "gate_w"), (gate_b[:, :], "gate_b")):
                sp.dma_start(dst, ins[name]).then_inc(w_in, 16)
            sp.wait_ge(setup_pool, 1)
            for layer in range(LAYERS):
                for b in range(2):
                    sp.dma_start(wo[64 * b:64 * b + 64, layer, b, :, :], ins["wo"][layer]).then_inc(w_in, 16)
            sp.dma_start(x[:, 4:TILES, :], xv[:, 4:TILES, :]).then_inc(x_in, 16)
            sp.dma_start(w1[:, :], ins["w1"]).then_inc(moe_in, 16)
            sp.dma_start(w2[:, :], ins["w2"]).then_inc(moe_in, 16)
            cv = ins["ctx"].rearrange("(u t r) s d -> u (r s) t d", r=2, t=TPU)
            for u in (0, 1):
                sp.dma_start(ctx_in[:, u, :, :], cv[u]).then_inc(ctx_sem[u], 16)
            with sp.Fori(1, UNITS // 2) as i:
                for par in (0, 1):
                    sp.wait_ge(ctx_used, 2 * i + (par - 1))
                    sp.dma_start(ctx_in[:, par, :, :], cv[2 * i + par]).then_inc(ctx_sem[par], 16)

            sp.wait_ge(setup_pool, 4)
            sp.dma_start(slots_in.rearrange("(t p) d -> p t d", p=P),
                         zero[:, None, :].broadcast_to([P, SLOT_TILES, DIM])).then_inc(zeroed, 16)
            sp.wait_ge(scattered, 16 * TILES)

            def step(s, least, r, lap):
                j = behind(s, least, 0, SLOT_TILES)
                if j is not None:
                    if least >= RING:
                        sp.wait_ge(e_xT, j - RING + 1)
                    sp.dma_start(xs[:, r, :], slots_in[bass.ds(P * j, P), :]).then_inc(e_in[r], 16)
                j = behind(s, least, 3, SLOT_TILES)
                if j is not None:
                    sp.wait_ge(e_y, j + 1)
                    sp.dma_start(slots_out[bass.ds(P * j, P), :], ys[:, r, :]).then_inc(e_out[r], 16)

            expert_pipeline(sp, step, 3)
            ov = out.rearrange("(t r) s d -> (r s) t d", r=2)
            for g in range(GROUPS):
                part = slice(g * TILES // GROUPS, (g + 1) * TILES // GROUPS)
                sp.wait_ge(summed, g + 1)
                sp.dma_start(ov[:, part, :], z[:, part, :]).then_inc(stored, 16)
            sp.wait_ge(stored, 16 * GROUPS)

        @block.gpsimd
        def _(pool):
            nc.gpsimd.memset(wo[:, :, :, :, :], 0.0).then_inc(setup_pool, 1)
            nc.gpsimd.memset(mhalf[:, :], -0.5).then_inc(setup_pool, 1)
            nc.gpsimd.memset(eps[:, :], EPS).then_inc(setup_pool, 1)
            nc.gpsimd.memset(zero[:, :], 0.0).then_inc(setup_pool, 1)
            pool.wait_ge(setup_pool, 4)
            pool.wait_ge(c_in, 16)

            def step(F, C, B, par):
                if F is None:
                    return
                n = F.n
                pool.wait_ge(d_mom, 2 * n + 2)
                nc.gpsimd.tensor_tensor(veps[:, :], mom[:, :, 1], eps[:, :], ALU.add).then_inc(g_veps, 1)
                pool.wait_ge(g_veps, n + 1)
                nc.gpsimd.tensor_tensor(rstd[:, :], veps[:, :], mhalf[:, :], ALU.pow).then_inc(g_rstd, 1)
                if F.layer == 2:
                    m = F.u
                    pool.wait_ge(d_mom2, 2 * m + 2)
                    nc.gpsimd.tensor_tensor(veps2[:, :], mom2[:, :, 1], eps[:, :], ALU.add).then_inc(g_veps2, 1)
                    pool.wait_ge(g_veps2, m + 1)
                    nc.gpsimd.tensor_tensor(rstd2[:, :], veps2[:, :], mhalf[:, :], ALU.pow).then_inc(g_rstd2, 1)
                pool.wait_ge(a_qk if F.layer else d_qk, n + 1 - (UNITS if F.layer else 0))
                if F.least > 1:
                    pool.wait_ge(p_s, 2 * n - 2)
                nc.gpsimd.tensor_tensor(km[:, par, 0, :], qkT[:, par, 1, :],
                                        const("head_mask")[:, 0:1].broadcast_to([P, COLS]), ALU.mult)
                for h in range(1, HEADS):
                    last = nc.gpsimd.tensor_scalar(km[:, par, h, :], qkT[:, par, 1, :], const("head_mask")[:, h:h + 1],
                                                   1.0, ALU.mult, ALU.mult)
                last.then_inc(g_km, 1)

            pipeline(pool, step)

            def gate_step(s, least, par):
                u = behind(s, least, 0, UNITS)
                if u is not None:
                    pool.wait_ge(r_mom, u + 1)
                    nc.gpsimd.tensor_tensor(gveps[:, par, :], gmom[:, par, :, 1], eps[:, :], ALU.add).then_inc(r_veps, 1)
                    pool.wait_ge(r_veps, u + 1)
                    nc.gpsimd.tensor_tensor(grstd[:, par, :], gveps[:, par, :], mhalf[:, :], ALU.pow).then_inc(r_rstd, 1)

            gate_pipeline(pool, gate_step)
            pool.wait_ge(zeroed, 16)
            pool.wait_ge(routed, 1)
            for t in range(TILES):
                nc.gpsimd.indirect_dma_start(out=slots_in, out_offset=bass.IndirectOffsetOnAxis(ap=slot[:, t:t + 1], axis=0),
                                             in_=z[:, t, :], in_offset=None).then_inc(scattered, 16)
            for r in range(RING):
                pool.wait_ge(e_out[r], 16 * SLOT_TILES // RING)
            for g in range(GROUPS):
                for t in range(g * TILES // GROUPS, (g + 1) * TILES // GROUPS):
                    nc.gpsimd.indirect_dma_start(out=z[:, t, :], out_offset=None, in_=slots_out,
                                                 in_offset=bass.IndirectOffsetOnAxis(ap=slot[:, t:t + 1], axis=0),
                                                 ).then_inc(gathered[g], 16)

        @block.scalar
        def _(act):
            def step(F, C, B, par):
                if B is not None:
                    n = B.n
                    act.wait_ge(p_pv, 2 * n + 2)
                    if B.least:
                        act.wait_ge(p_t1, n)
                    nc.scalar.activation(oT[:, :], pv_ps, ACT.Copy).then_inc(a_oT, 1)
                if F is not None:
                    n = F.n
                    act.wait_ge(p_xT, n + 1)
                    if F.least:
                        act.wait_ge(p_v, n)
                    if F.layer == 2:
                        nc.scalar.activation(xT[:, :], m0[:, 0:COLS], ACT.Identity, bias=cols[:, 3:4],
                                             scale=cols[:, 2:3]).then_inc(a_xT, 1)
                    elif F.layer == 1:
                        nc.scalar.activation(cT[:, :], m0[:, COLS:2 * COLS], ACT.Copy)
                        nc.scalar.activation(xT[:, :], m0[:, 0:COLS], ACT.Copy).then_inc(a_xT, 1)
                    else:
                        nc.scalar.activation(xT[:, :], m0[:, 0:COLS], ACT.Copy).then_inc(a_xT, 1)
                if F is not None and F.layer:
                    act.wait_ge(p_qk, n + 1)
                    act.wait_ge(p_st, 2 * n - 2)
                    act.wait_ge(d_qm, n - 1)
                    act.wait_ge(g_km, n - 1)
                    if F.layer == 1:
                        for i in range(2):
                            last = nc.scalar.activation(qkT[:, par, i, :], m1[:, i * COLS:(i + 1) * COLS], ACT.Identity,
                                                        bias=cols[:, i:i + 1])
                    else:
                        last = nc.scalar.activation(qkT[:, par, :, :].rearrange("p a c -> p (a c)"), m1, ACT.Copy)
                    last.then_inc(a_qk, 1)
                if B is not None:
                    n = B.n
                    act.wait_ge(p_t2, n + 1)
                    if B.least:
                        act.wait_ge(p_out, n)
                    nc.scalar.activation(hT[:, :], m2[:, 0:COLS], ACT.Copy).then_inc(a_hT, 1)
                if C is not None:
                    n = C.n
                    for t in range(TPU):
                        act.wait_ge(p_st, 2 * n + t + 1)
                        if C.least:
                            act.wait_ge(p_pv, 2 * n - 1 + t)
                        nc.scalar.activation(prob[:, t, :], st_ps, ACT.Exp, scale=SCALE).then_inc(a_exp, 1)

            act.wait_ge(w_in, 16 * 13)
            pipeline(act, step)

            def gate_step(s, least, par):
                u = behind(s, least, 2, UNITS)
                if u is not None:
                    act.wait_ge(r_zn, u + 1)
                    nc.scalar.activation(z[:, bass.ds(TPU * u, TPU), :], zn[:, par, :, :], ACT.Copy)
                    act.wait_ge(r_zT, u + 1)
                    nc.scalar.activation(zT[:, par, :], (m0, m1)[par][:, 0:COLS], ACT.Identity, bias=cols[:, 5:6],
                                         scale=cols[:, 4:5]).then_inc(r_zT_sb, 1)

            gate_pipeline(act, gate_step)

            def expert_step(s, least, r, lap):
                j = behind(s, least, 0, SLOT_TILES)
                if j is not None:
                    act.wait_ge(e_xT, j + 1)
                    nc.scalar.activation(xsT[:, r, :], psum[:, 6, 0:P], ACT.Identity, bias=cols[:, 5:6],
                                         scale=cols[:, 4:5]).then_inc(e_xT_sb, 1)
                j = behind(s, least, 1, SLOT_TILES)
                if j is not None:
                    q = (r - 1) % RING
                    act.wait_ge(e_up, j + 1)
                    nc.scalar.activation(hs[:, q, :], psum[:, q, :], ACT.Gelu_apprx_tanh).then_inc(e_gelu, 1)

            expert_pipeline(act, expert_step, 1)

        @block.vector
        def _(dve):
            nc.vector.memset(vb[:, :, :, :, :], 0.0).then_inc(alibi_step, 1)
            nc.vector.memset(mx[:, :, :, :, :], 0.0).then_inc(alibi_step, 1)
            nc.vector.memset(pv_ps, 0.0)
            dve.wait_ge(alibi_step, 1)
            nc.vector.memset(vb[0:64, :, :, :, 16:17], 1.0)
            nc.vector.memset(vb[64:128, :, :, :, 17:18], 1.0).then_inc(setup, 1)
            dve.wait_ge(c_in, 16)
            nc.vector.tensor_copy(pick16[:, :], const("pick"))
            nc.vector.tensor_copy(pickbf[:, :], const("pick")[:, 0:SEQ])
            nc.vector.tensor_copy(sel[:, 0, :], const("sel0"))
            nc.vector.tensor_copy(sel[:, 1, :], const("sel1")).then_inc(setup, 1)
            dve.wait_ge(w_in, 16 * 13)
            big = qm_flat[:, 0:HEADS * SEQ].rearrange("p (h s) -> p h s", h=HEADS)
            done = 2
            for dist, table in (("dist_qk", alibi_qk), ("dist_kq", alibi_kq)):
                nc.vector.tensor_tensor(big, const(dist)[:, None, :].broadcast_to([P, HEADS, SEQ]),
                                        slopes[:, :, None].broadcast_to([P, HEADS, SEQ]), ALU.mult).then_inc(alibi_step, 1)
                dve.wait_ge(alibi_step, done + 1)
                nc.vector.tensor_copy(table[:, :, :], big).then_inc(alibi_step, 1)
                dve.wait_ge(alibi_step, done + 2)
                nc.vector.tensor_tensor(table[64:128, :, :], big[64:128, :, :], table[64:128, :, :],
                                        ALU.subtract).then_inc(alibi_step, 1)
                done += 3
                dve.wait_ge(alibi_step, done)

            def step(F, C, B, par):
                first = F is not None and F.least == 0
                if F is not None:
                    n = F.n
                    if F.layer == 0:
                        dve.wait_ge(x_in, 16 if F.least < 2 else 32)
                    else:
                        dve.wait_ge(d_res, n - UNITS + 1)
                    if not first:
                        dve.wait_ge(g_veps, n)
                        nc.vector.memset(carrier[:, :], 0.0)
                    for t in range(TPU):
                        nc.vector.bn_stats(stats[:, t, :], x[:, TPU * F.u + t, :]).then_inc(d_stats, 1)
                    dve.wait_ge(d_stats, 2 * n + 2)
                    nc.vector.memset(carrier[:, :], 0.0)
                    for t in range(TPU):
                        nc.vector.bn_aggr(mom[:, t, :], stats[:, t, :]).then_inc(d_mom, 1)
                if C is not None:
                    c = C.n
                    dve.wait_ge(p_s, 2 * c + 1)
                    if C.least:
                        dve.wait_ge(d_mx, c)
                    nc.vector.tensor_reduce(mrow[:, 0, :], s_ps.rearrange("p (h s) -> p h s", h=HEADS), AX.X,
                                            ALU.max).then_inc(d_max, 1)
                if F is not None:
                    dve.wait_ge(g_rstd, n + 1)
                    if not first:
                        dve.wait_ge(p_xT, n)
                    dst = (lambda t: y[:, TPU * F.u + t, :]) if F.layer == 2 else (lambda t: xn[:, t, :])
                    for t in range(TPU):
                        last = nc.vector.tensor_scalar(dst(t), x[:, TPU * F.u + t, :], mom[:, t, 0:1], rstd[:, t:t + 1],
                                                       ALU.subtract, ALU.mult)
                    if F.layer != 2:
                        last.then_inc(d_xn, 1)
                    else:
                        m = F.u
                        last.then_inc(d_y, 1)
                        dve.wait_ge(d_y, m + 1)
                        nc.vector.memset(carrier[:, :], 0.0)
                        for t in range(TPU):
                            nc.vector.bn_stats(stats2[:, t, :], y[:, TPU * F.u + t, :]).then_inc(d_stats2, 1)
                        dve.wait_ge(d_stats2, 2 * m + 2)
                        nc.vector.memset(carrier[:, :], 0.0)
                        for t in range(TPU):
                            nc.vector.bn_aggr(mom2[:, t, :], stats2[:, t, :]).then_inc(d_mom2, 1)
                if C is not None:
                    dve.wait_ge(p_s, 2 * c + 2)
                    nc.vector.tensor_reduce(mrow[:, 1, :], s_ps.rearrange("p (h s) -> p h s", h=HEADS), AX.X,
                                            ALU.max).then_inc(d_max, 1)
                if F is not None and F.layer == 2:
                    dve.wait_ge(g_rstd2, m + 1)
                    for t in range(TPU):
                        last = nc.vector.tensor_scalar(xn[:, t, :], y[:, TPU * F.u + t, :], mom2[:, t, 0:1],
                                                       rstd2[:, t:t + 1], ALU.subtract, ALU.mult)
                    last.then_inc(d_xn, 1)
                if C is not None:
                    dve.wait_ge(d_max, 2 * c + 2)
                    if C.least:
                        dve.wait_ge(p_mT, c)
                    for b in range(2):
                        part = slice(64 * b, 64 * b + 64)
                        last = nc.vector.tensor_scalar(mx[part, :, b, 0, :], mrow[part, :, :], -1.0, None, ALU.mult)
                    last.then_inc(d_mhi, 1)
                    dve.wait_ge(d_mhi, c + 1)
                    for b in range(2):
                        part = slice(64 * b, 64 * b + 64)
                        last = nc.vector.scalar_tensor_tensor(out=mx[part, :, b, 1, :], in0=mrow[part, :, :], scalar=-1.0,
                                                              in1=mx[part, :, b, 0, :], op0=ALU.mult, op1=ALU.subtract)
                    last.then_inc(d_mx, 1)
                if B is not None:
                    b_ = B.n
                    dve.wait_ge(p_t1, b_ + 1)
                    t1 = m2.rearrange("p (t g w) -> p t g w", t=TPU, g=HALF)
                    nc.vector.reciprocal(rc[:, :, :], m2.rearrange("p (g w) -> p g w", w=32)[:, :, 16:18]).then_inc(d_rc, 1)
                    dve.wait_ge(d_rc, b_ + 1)
                    if B.least:
                        dve.wait_ge(p_t2, b_)
                    for t in range(TPU):
                        last = nc.vector.tensor_tensor(
                            on[:, t, :, :, :].rearrange("p b g d -> p g b d"),
                            t1[:, t, :, 0:16].rearrange("p g (b d) -> p g b d", b=2),
                            rc[:, t * HALF:(t + 1) * HALF, :][:, :, :, None].broadcast_to([P, HALF, 2, HD]), ALU.mult)
                    last.then_inc(d_on, 1)
                if C is not None:
                    dve.wait_ge(p_mT, c + 1)
                    if C.least:
                        dve.wait_ge(p_st, 2 * c)
                    nc.vector.tensor_tensor(mb[:, :, :], st_ps[:, 0:SEQ][:, None, :].broadcast_to([P, HEADS, SEQ]),
                                            const("mb_mask")[:, :, None].broadcast_to([P, HEADS, SEQ]),
                                            ALU.mult).then_inc(d_mb, 1)
                if F is not None:
                    if F.layer == 0:
                        dve.wait_ge(p_qk, n + 1)
                        tab = lambda name: const(name)[:, None, :].broadcast_to([P, 2 * COLS // SEQ, SEQ])
                        blocks = lambda ap: ap.rearrange("p (b s) -> p b s", s=SEQ)
                        if not first:
                            dve.wait_ge(d_qk, n)
                        nc.vector.tensor_tensor(blocks(rope_a[:, :]), blocks(m1), tab("cos"), ALU.mult).then_inc(d_rope, 1)
                        dve.wait_ge(p_rot, n + 1)
                        nc.vector.tensor_tensor(blocks(rope_b[:, :]), blocks(m0), tab("sin"), ALU.mult).then_inc(d_rope, 1)
                        dve.wait_ge(d_rope, 2 * n + 2)
                        if F.least > 1:
                            dve.wait_ge(p_st, 2 * n - 2)
                            dve.wait_ge(g_km, n - 1)
                        nc.vector.tensor_tensor(qkT[:, par, :, :].rearrange("p a c -> p (a c)"), rope_a[:, :], rope_b[:, :],
                                                ALU.add).then_inc(d_qk, 1)
                if B is not None:
                    dve.wait_ge(p_out, b_ + 1)
                    o = m2[:, COLS:2 * COLS].rearrange("p (t d) -> p t d", t=TPU)
                    res = x if B.layer < 2 else y
                    here = res[:, bass.ds(TPU * B.u, TPU), :]
                    if B.layer < 2:
                        nc.vector.tensor_tensor(delta[:, :, :], o, rows[:, B.layer, None, :].broadcast_to([P, TPU, DIM]),
                                                ALU.add).then_inc(d_delta, 1)
                        dve.wait_ge(d_delta, b_ + 1)
                        nc.vector.tensor_tensor(here, here, delta[:, :, :], ALU.add).then_inc(d_res, 1)
                    else:
                        nc.vector.tensor_tensor(here, here, o, ALU.add).then_inc(d_res, 1)
                if F is not None:
                    dve.wait_ge(d_qk, n + 1) if F.layer == 0 else dve.wait_ge(a_qk, n - UNITS + 1)
                    if F.least > 1:
                        dve.wait_ge(p_st, 2 * n - 2)
                    for h in range(HEADS):
                        last = nc.vector.tensor_scalar(qm[:, par, h, :], qkT[:, par, 0, :], const("head_mask")[:, h:h + 1],
                                                       None, ALU.mult)
                    last.then_inc(d_qm, 1)
                    dve.wait_ge(p_v, n + 1)
                    if F.least > 1:
                        dve.wait_ge(p_pv, 2 * n - 2)
                    for b in range(2):
                        part = slice(64 * b, 64 * b + 64)
                        src = m0[part, 0:COLS].rearrange("p (t h d) -> p t h d", t=TPU, h=HEADS)
                        dst = vb[part, par, :, :, 8 * b:8 * b + 8]
                        if F.layer == 1:
                            for t in range(TPU):
                                last = nc.vector.tensor_tensor(dst[:, t], src[:, t],
                                                               rows[part, 2, :].rearrange("p (h d) -> p h d", h=HEADS), ALU.add)
                        else:
                            last = nc.vector.tensor_copy(dst, src)
                    last.then_inc(d_v, 1)

            pipeline(dve, step)

            nc.vector.tensor_copy(before[:, :], const("before"))
            nc.vector.memset(ones[:, :], 1.0)
            dve.wait_ge(d_res, LAYERS * UNITS)
            nc.vector.memset(carrier[:, :], 0.0)

            def gate_step(s, least, par):
                u = behind(s, least, 0, UNITS)
                if u is not None:
                    for t in range(TPU):
                        nc.vector.bn_stats(gstats[:, par, t, :], y[:, TPU * u + t, :]).then_inc(r_stats, 1)
                    dve.wait_ge(r_stats, 2 * u + 2)
                    if least >= 2:
                        dve.wait_ge(r_zn, u - 1)
                    nc.vector.memset(carrier[:, :], 0.0)
                    for t in range(TPU):
                        last = nc.vector.bn_aggr(gmom[:, par, t, :], gstats[:, par, t, :])
                    last.then_inc(r_mom, 1)
                u = behind(s, least, 1, UNITS)
                if u is not None:
                    dve.wait_ge(r_rstd, u + 1)
                    if least >= 3:
                        dve.wait_ge(r_zT_sb, u - 1)
                    for t in range(TPU):
                        last = nc.vector.tensor_scalar(zn[:, 1 - par, t, :], y[:, TPU * u + t, :],
                                                       gmom[:, 1 - par, t, 0:1], grstd[:, 1 - par, t:t + 1],
                                                       ALU.subtract, ALU.mult)
                    last.then_inc(r_zn, 1)
                u = behind(s, least, 3, UNITS)
                if u is not None:
                    dve.wait_ge(r_logits, u + 1)
                    nc.vector.tensor_tensor(logits[:, bass.ds(TPU * u, TPU), :],
                                            (m0, m1)[1 - par][:, COLS:COLS + TPU * EXPERTS].rearrange("p (t e) -> p t e", t=TPU),
                                            gate_b[:, None, :].broadcast_to([P, TPU, EXPERTS]), ALU.add).then_inc(r_biased, 1)

            gate_pipeline(dve, gate_step)

            TE = [P, TILES, EXPERTS]
            by_tile = lambda a: a[:, :, None].broadcast_to(TE)
            by_expert = lambda a: a[:, None, :].broadcast_to(TE)
            dve.wait_ge(r_biased, UNITS)
            nc.vector.tensor_reduce(best, logits, AX.X, ALU.max).then_inc(route, 1)
            dve.wait_ge(route, 1)
            nc.vector.tensor_tensor(tie, logits, by_tile(best), ALU.is_ge).then_inc(route, 1)
            dve.wait_ge(route, 2)
            nc.vector.tensor_tensor(tie, tie, by_expert(const("first")), ALU.mult).then_inc(route, 1)
            dve.wait_ge(route, 3)
            nc.vector.tensor_reduce(tie_best, tie, AX.X, ALU.max).then_inc(route, 1)
            dve.wait_ge(route, 4)
            nc.vector.tensor_tensor(onehot[:, :, :], tie, by_tile(tie_best), ALU.is_equal).then_inc(route, 1)
            in_tile = psum[:, 0, 0:TILES * EXPERTS].rearrange("p (t e) -> p t e", t=TILES)
            total = psum[:, 1, 0:TILES * EXPERTS].rearrange("p (t e) -> p t e", t=TILES)
            dve.wait_ge(counted, 2)
            nc.vector.tensor_copy(count[:, 0, :, :], total).then_inc(route, 1)
            done, now, shift = 6, 0, 1
            while shift < TILES:
                dve.wait_ge(route, done)
                nc.vector.tensor_copy(count[:, 1 - now, 0:shift, :], count[:, now, 0:shift, :])
                nc.vector.tensor_tensor(count[:, 1 - now, shift:TILES, :], count[:, now, shift:TILES, :],
                                        count[:, now, 0:TILES - shift, :], ALU.add).then_inc(route, 1)
                done, now, shift = done + 1, 1 - now, 2 * shift
            upto_tile = count[:, now, :, :]
            dve.wait_ge(route, done)
            nc.vector.tensor_tensor(filled, upto_tile[:, TILES - 1, :, None].broadcast_to([P, EXPERTS, TILES]),
                                    const("slot128")[:, None, :].broadcast_to([P, EXPERTS, TILES]),
                                    ALU.is_gt).then_inc(route, 1)
            nc.vector.tensor_tensor(place[:, 0, :, :], in_tile, upto_tile, ALU.add)
            dve.wait_ge(route, done + 1)
            nc.vector.tensor_reduce(used, filled, AX.X, ALU.add).then_inc(route, 1)
            dve.wait_ge(route, done + 2)
            nc.vector.tensor_copy(ends[:, 0, :], used).then_inc(route, 1)
            nc.vector.tensor_tensor(place[:, 1, :, :], place[:, 0, :, :], total, ALU.subtract)
            done, now, shift = done + 3, 0, 1
            while shift < EXPERTS:
                dve.wait_ge(route, done)
                nc.vector.tensor_copy(ends[:, 1 - now, 0:shift], ends[:, now, 0:shift])
                nc.vector.tensor_tensor(ends[:, 1 - now, shift:EXPERTS], ends[:, now, shift:EXPERTS],
                                        ends[:, now, 0:EXPERTS - shift], ALU.add).then_inc(route, 1)
                done, now, shift = done + 1, 1 - now, 2 * shift
            last_tile = ends[:, now, :]
            dve.wait_ge(route, done)
            nc.vector.tensor_tensor(base, last_tile, used, ALU.subtract).then_inc(route, 1)
            nc.vector.tensor_tensor(passed, const("tile_no")[:, :, None].broadcast_to([P, SLOT_TILES, EXPERTS]),
                                    last_tile[:, None, :].broadcast_to([P, SLOT_TILES, EXPERTS]), ALU.is_ge).then_inc(route, 1)
            dve.wait_ge(route, done + 2)
            nc.vector.scalar_tensor_tensor(out=place[:, 2, :, :], in0=by_expert(base), scalar=float(P),
                                           in1=place[:, 1, :, :], op0=ALU.mult, op1=ALU.add).then_inc(route, 1)
            nc.vector.tensor_reduce(expert_f, passed, AX.X, ALU.add).then_inc(route, 1)
            dve.wait_ge(route, done + 4)
            nc.vector.tensor_tensor(place[:, 0, :, :], place[:, 2, :, :], onehot[:, :, :], ALU.mult).then_inc(route, 1)
            nc.vector.tensor_scalar(expert[:, :], expert_f, float(EXPERTS - 1), float(HID), ALU.min, ALU.mult)
            dve.wait_ge(route, done + 5)
            nc.vector.tensor_reduce(slot_f, place[:, 0, :, :], AX.X, ALU.add).then_inc(route, 1)
            dve.wait_ge(route, done + 6)
            nc.vector.tensor_scalar(slot[:, :], slot_f, float(SLOT_TILES * P - 1), None, ALU.min).then_inc(routed, 1)
            nc.vector.tensor_tensor(x[:, :, :], x[:, :, :], y[:, :, :], ALU.add).then_inc(xy_sum, 1)

            def expert_step(s, least, r, lap):
                j = behind(s, least, 2, SLOT_TILES)
                if j is not None:
                    q = (r - 2) % RING
                    dve.wait_ge(e_hT, j + 1)
                    nc.vector.tensor_copy(hsT[:, q, :], psum[:, q, :]).then_inc(e_hT_sb, 1)
                    dve.wait_ge(e_down, j + 1)
                    if least - 2 >= RING:
                        dve.wait_ge(e_out[q], 16 * (lap + (r - 2) // RING))
                    nc.vector.tensor_copy(ys[:, q, :], psum[:, 3 + q, P:2 * P]).then_inc(e_y, 1)

            expert_pipeline(dve, expert_step, 2)
            dve.wait_ge(xy_sum, 1)
            for g in range(GROUPS):
                part = slice(g * TILES // GROUPS, (g + 1) * TILES // GROUPS)
                dve.wait_ge(gathered[g], 16 * TILES // GROUPS)
                nc.vector.tensor_tensor(z[:, part, :], z[:, part, :], x[:, part, :], ALU.add).then_inc(summed, 1)

        @block.tensor
        def _(pe):
            mm = nc.tensor.matmul

            def scores(C, t, par, into, stationary, spread, start):
                for half in range(2):
                    for b in range(2):
                        last = mm(into[64 * b:64 * b + 64, half * 512:(half + 1) * 512],
                                  stationary[:, tok(t, b)], spread[:, half * HALF:(half + 1) * HALF, tok(t, b)],
                                  start=start, stop=True, skip_group_check=True)
                return last

            def alibi(into, table, start):
                for half in range(2):
                    mm(into[:, half * 512:(half + 1) * 512], pick16[:, :], table[:, half * HALF:(half + 1) * HALF, :],
                       start=start, stop=False, skip_group_check=True)

            def values(U, t, par):
                n = U.n
                pe.wait_ge(a_exp, 2 * n + t + 1)
                if t == 0:
                    pe.wait_ge(d_v, n + 1)
                    if U.least:
                        pe.wait_ge(a_oT, n)
                for h in range(HEADS):
                    c, g = h % 4, h // 4
                    last = mm(pv_ps[32 * c:32 * c + 18, (4 * t + g) * SEQ:(4 * t + g + 1) * SEQ], vb[:, par, t, h, :],
                              prob[:, t, h * SEQ:(h + 1) * SEQ], start=True, stop=True, tile_position=(0, 32 * c))
                last.then_inc(p_pv, 1)

            def score_max(C, t, par):
                n = C.n
                if t == 0:
                    pe.wait_ge(g_km, n + 1)
                if t or C.least:
                    pe.wait_ge(d_max, 2 * n + t)
                if C.layer == 0:
                    alibi(s_ps, alibi_qk, True)
                scores(C, t, par, s_ps, qkT[:, par, 0, :], km[:, par, :, :], C.layer != 0).then_inc(p_s, 1)

            def score_exp(C, t, par):
                n = C.n
                if t == 0:
                    pe.wait_ge(d_mb, n + 1)
                    pe.wait_ge(d_qm, n + 1)
                else:
                    pe.wait_ge(a_exp, 2 * n + t)
                for half in range(2):
                    mm(st_ps[:, half * 512:(half + 1) * 512], sel[:, t, :], mb[:, half * HALF:(half + 1) * HALF, :],
                       start=True, stop=False, skip_group_check=True)
                if C.layer == 0:
                    alibi(st_ps, alibi_kq, False)
                scores(C, t, par, st_ps, qkT[:, par, 1, :], qm[:, par, :, :], False).then_inc(p_st, 1)

            def step(F, C, B, par):
                cpar = 1 - par
                if C is not None:
                    score_max(C, 0, cpar)
                if B is not None:
                    values(B, 1, par)
                if C is not None:
                    score_max(C, 1, cpar)
                if F is not None:
                    n = F.n
                    pe.wait_ge(d_xn, n + 1)
                    if F.least:
                        pe.wait_ge(d_v, n)
                    if F.layer == 1:
                        pe.wait_ge(ctx_sem[par], 8 * (F.u - par) + 16)
                        for t in range(TPU):
                            last = mm(m0[:, COLS + t * P:COLS + (t + 1) * P], ctx_in[:, par, t, :], ident,
                                      is_transpose=True, start=True, stop=True)
                        last.then_inc(ctx_used, 1)
                    for t in range(TPU):
                        last = mm(m0[:, t * P:(t + 1) * P], xn[:, t, :], ident, is_transpose=True, start=True, stop=True)
                    last.then_inc(p_xT, 1)
                if B is not None:
                    b_ = B.n
                    pe.wait_ge(a_oT, b_ + 1)
                    if B.least:
                        pe.wait_ge(d_res, b_)
                    for k in range(2 * TPU):
                        last = mm(m2[:, k * P:(k + 1) * P], oT[:, k * P:(k + 1) * P], ident, is_transpose=True,
                                  start=True, stop=True)
                    last.then_inc(p_t1, 1)
                if F is not None:
                    pe.wait_ge(a_xT, n + 1)
                    if F.least:
                        if F.layer == 0:
                            pe.wait_ge(d_rope, 2 * n)
                        elif F.least == UNITS:
                            pe.wait_ge(d_rope, 2 * n)
                        else:
                            pe.wait_ge(a_qk, n - UNITS)
                    for i in range(2):
                        last = mm(m1[:, i * COLS:(i + 1) * COLS], wqkv[:, F.layer, i, :],
                                  cT[:, :] if i and F.layer == 1 else xT[:, :], start=True, stop=True)
                    last.then_inc(p_qk, 1)
                    if F.layer == 0:
                        for i in range(2):
                            last = mm(m0[:, i * COLS:(i + 1) * COLS], wrot[:, i, :], xT[:, :], start=True, stop=True)
                        last.then_inc(p_rot, 1)
                if B is not None:
                    pe.wait_ge(d_on, b_ + 1)
                    for t in range(TPU):
                        last = mm(m2[:, t * P:(t + 1) * P], on[:, t, :, :, :].rearrange("p b g d -> p (b g d)"), ident,
                                  is_transpose=True, start=True, stop=True)
                    last.then_inc(p_t2, 1)
                if C is not None:
                    c = C.n
                    pe.wait_ge(d_mx, c + 1)
                    if C.least:
                        pe.wait_ge(a_exp, 2 * c)
                    mm(st_ps[:, 0:SEQ], mx[:, :, :, :, :].rearrange("p t b l h -> p (t b l h)"), pickbf[:, :],
                       start=True, stop=True).then_inc(p_mT, 1)
                if B is not None:
                    pe.wait_ge(a_hT, b_ + 1)
                    for t in range(TPU):
                        for g2 in range(2):
                            for b in range(2):
                                last = mm(m2[64 * b:64 * b + 64, COLS + t * P:COLS + (t + 1) * P],
                                          hT[:, t * P + g2 * SEQ:t * P + (g2 + 1) * SEQ], wo[:, B.layer, b, g2, :],
                                          start=g2 == 0, stop=g2 == 1, skip_group_check=True)
                    last.then_inc(p_out, 1)
                if C is not None:
                    score_exp(C, 0, cpar)
                if F is not None:
                    if F.layer == 0:
                        pe.wait_ge(d_rope, 2 * n + 2)
                    for t in range(TPU):
                        last = mm(m0[:, t * P:(t + 1) * P], (cT if F.layer == 1 else xT)[:, t * P:(t + 1) * P],
                                  wqkv[:, F.layer, 2, :], start=True, stop=True)
                    last.then_inc(p_v, 1)
                if C is not None:
                    score_exp(C, 1, cpar)
                    values(C, 0, cpar)

            pe.wait_ge(c_in, 16)
            pe.wait_ge(w_in, 16 * 13)
            pe.wait_ge(setup, 2)
            pe.wait_ge(alibi_step, 8)
            pipeline(pe, step)

            def gate_step(s, least, par):
                u = behind(s, least, 3, UNITS)
                if u is not None:
                    bank = (m0, m1)[1 - par]
                    pe.wait_ge(r_zT_sb, u + 1)
                    for t in range(TPU):
                        last = mm(bank[:, COLS + t * EXPERTS:COLS + (t + 1) * EXPERTS], zT[:, 1 - par, t * P:(t + 1) * P],
                                  gate_w[:, :], start=True, stop=True)
                    last.then_inc(r_logits, 1)
                u = behind(s, least, 2, UNITS)
                if u is not None:
                    pe.wait_ge(r_zn, u + 1)
                    if least >= 4:
                        pe.wait_ge(r_biased, u - 1)
                    for t in range(TPU):
                        last = mm((m0, m1)[par][:, t * P:(t + 1) * P], zn[:, par, t, :], ident, is_transpose=True,
                                  start=True, stop=True)
                    last.then_inc(r_zT, 1)

            gate_pipeline(pe, gate_step)
            pe.wait_ge(route, 5)
            for k, rows_used in enumerate((before, ones)):
                mm(psum[:, k, 0:TILES * EXPERTS], rows_used[:, :], onehot[:, :, :], start=True, stop=True).then_inc(counted, 1)

            def weight_column(j):
                return pe.value_load(expert[0:1, bass.ds(j, 1)], min_val=0, max_val=(EXPERTS - 1) * HID)

            def expert_step(s, least, r, lap):
                j = behind(s, least, 2, SLOT_TILES)
                q = (r - 2) % RING
                if j is not None:
                    pe.wait_ge(e_gelu, j + 1)
                    for c in range(CHUNKS):
                        last = mm(psum[:, q, c * P:(c + 1) * P], hs[:, q, c * P:(c + 1) * P], ident, is_transpose=True,
                                  start=True, stop=True)
                    last.then_inc(e_hT, 1)
                i = behind(s, least, 1, SLOT_TILES)
                if i is not None:
                    k = (r - 1) % RING
                    col = weight_column(i)
                    pe.wait_ge(e_xT_sb, i + 1)
                    if least - 1 >= RING:
                        pe.wait_ge(e_hT_sb, i - RING + 1)
                    mm(psum[:, k, :], xsT[:, k, :], w1[:, bass.ds(col, HID)], start=True, stop=True).then_inc(e_up, 1)
                i = behind(s, least, 0, SLOT_TILES)
                if i is not None:
                    pe.wait_ge(e_in[r], 16 * (lap + 1))
                    mm(psum[:, 6, 0:P], xs[:, r, :], ident, is_transpose=True, start=True, stop=True).then_inc(e_xT, 1)
                if j is not None:
                    col = weight_column(j)
                    pe.wait_ge(e_hT_sb, j + 1)
                    if least - 2 >= RING:
                        pe.wait_ge(e_y, j - RING + 1)
                    for c in range(CHUNKS):
                        last = mm(psum[:, 3 + q, P:2 * P], hsT[:, q, c * P:(c + 1) * P], w2[:, bass.ds(col + c * P, P)],
                                  start=c == 0, stop=c == CHUNKS - 1)
                    last.then_inc(e_down, 1)

            pe.wait_ge(routed, 1)
            pe.wait_ge(moe_in, 32)
            expert_pipeline(pe, expert_step, 2)


def constants(np):
    c = np.zeros((P, CONST_COLS), np.float32)

    def put(name, a):
        lo, hi = CONST[name]
        c[:, lo:hi] = a
    p = np.arange(P)
    put("ident", np.eye(P))
    put("pick", np.tile(np.eye(64), (2, 2)))
    put("head_mask", p[:, None] // HD == np.arange(HEADS))
    put("mb_mask", p[:, None] % HEADS == np.arange(HEADS))
    for t in range(TPU):
        put(f"sel{t}", (p[:, None] // 32) == 2 * t + p[None, :] // 64)
    q = np.arange(SEQ)
    dist = np.minimum(q[None, :] - q[:, None], 0) * (8.0 / SCALE)
    put("dist_qk", np.tile(dist, (2, 1)))
    put("dist_kq", np.tile(dist.T, (2, 1)))
    inv = (1.0 / 10000.0 ** (np.arange(0, HD, 2, dtype=np.float32) / HD)).astype(np.float32)
    ang = (q.astype(np.float32)[:, None] * inv[None, :]).astype(np.float32)
    put("cos", np.cos(ang).T[p % 4])
    put("sin", np.sin(ang).T[p % 4] * np.where(p % HD < 4, -1.0, 1.0)[:, None])
    put("before", p[:, None] < p[None, :])
    put("first", np.broadcast_to(EXPERTS - np.arange(EXPERTS), (P, EXPERTS)))
    put("slot128", np.broadcast_to(P * np.arange(TILES), (P, TILES)))
    put("tile_no", np.broadcast_to(np.arange(SLOT_TILES), (P, SLOT_TILES)))
    return c


def kernel(**inputs):
    import numpy as np
    import concourse.bacc as bacc
    from concourse.bass_utils import run_bass_kernel_spmd

    a = {k: np.asarray(v) for k, v in inputs.items()}

    def heads_apart(w):
        return w.reshape(2, 2, 32, DIM).transpose(0, 2, 1, 3).reshape(64, 2 * DIM)

    qkv = a["L0_attn_qkv_w"].T
    rotated = np.arange(DIM) // HD * HD + (np.arange(DIM) + HD // 2) % HD
    every = lambda v: np.broadcast_to(v, (P, v.shape[-1]))
    arrays = {
        "consts": constants(np),
        "x": a["x"], "ctx": a["ctx_1024"],
        "wqkv": np.concatenate([qkv, a["L0_xattn_Wq"].T, a["L0_xattn_Wk"].T, a["L0_xattn_Wv"].T, a["L0_ffn_w_qkv"]], 1),
        "wrot": np.concatenate([qkv[:, rotated], qkv[:, DIM + rotated]], 1),
        "wo": np.stack([heads_apart(w) for w in (a["L0_attn_proj_w"].T, a["L0_xattn_Wo"].T, a["L0_ffn_w_proj"])]),
        "cols": np.stack([a["L0_xattn_bq"], a["L0_xattn_bk"], a["L0_ffn_ln1_w"], a["L0_ffn_ln1_b"],
                          a["L0_ffn_ln2_w"], a["L0_ffn_ln2_b"]], 1),
        "rows": np.concatenate([every(a[k]) for k in ("L0_attn_proj_b", "L0_xattn_bo", "L0_xattn_bv")], 1),
        "slopes": every(a["L0_attn_slopes"]),
        "gate_w": a["L0_ffn_gate_w"], "gate_b": every(a["L0_ffn_gate_b"]),
        "w1": a["L0_ffn_w1"].transpose(1, 0, 2).reshape(P, EXPERTS * HID),
        "w2": a["L0_ffn_w2"].reshape(EXPERTS, CHUNKS, P, DIM).transpose(2, 0, 1, 3).reshape(P, EXPERTS * HID),
    }
    arrays = {k: np.ascontiguousarray(v) for k, v in arrays.items()}
    nc = bacc.Bacc("TRN2", target_bir_lowering=False, num_devices=1)
    ins = {k: nc.dram_tensor(f"in_{k}", v.shape, mybir.dt.from_np(v.dtype), kind="ExternalInput").ap()
           for k, v in arrays.items()}
    out = nc.dram_tensor("out_x", (SEQS, SEQ, DIM), F32, kind="ExternalOutput").ap()
    slots_in = nc.dram_tensor("slots_in", (SLOT_TILES * P, DIM), F32, kind="Internal").ap()
    slots_out = nc.dram_tensor("slots_out", (SLOT_TILES * P, DIM), F32, kind="Internal").ap()
    decoder(nc, ins, out, slots_in, slots_out)
    r = run_bass_kernel_spmd(nc, [{f"in_{k}": v for k, v in arrays.items()}], core_ids=[0])
    return r.results[0]["out_x"]
```

```python
import concourse.bass as bass
from concourse import mybir
from collections import namedtuple
from contextlib import ExitStack

F32 = mybir.dt.float32
BF16 = mybir.dt.bfloat16
F16 = mybir.dt.float16
I32 = mybir.dt.int32
ALU = mybir.AluOpType
ACT = mybir.ActivationFunctionType
AX = mybir.AxisListType

P = 128
SEQS, SEQ, DIM, HEADS, HD = 64, 64, 128, 16, 8
TOKENS = SEQS * SEQ
TILES = TOKENS // P
TPU = 2
UNITS = TILES // TPU
COLS = TPU * P
LAYERS = 3
EPS = 1e-5
SCALE = HD ** -0.5
HALF = HEADS // 2
PAIRS = HEADS // 2
EXPERTS, HID = 8, 512
POOL_HEADS = 11
CHUNKS = HID // P
SLOT_TILES = (TOKENS - EXPERTS) // P + EXPERTS
RING = 3
WEIGHTS = 9
GROUPS = 4
assert SLOT_TILES % RING == 0

Unit = namedtuple("Unit", "layer u n least")

CONST = {}
CONST_COLS = 0
for _name, _n in (("ident", P), ("pick", P), ("head_mask", HEADS), ("dist_qk", SEQ), ("cos", SEQ), ("sin", SEQ), ("before", P),
                  ("first", EXPERTS), ("slot128", TILES), ("tile_no", SLOT_TILES)):
    CONST[_name] = (CONST_COLS, CONST_COLS + _n)
    CONST_COLS += _n


def decoder(nc, ins, out, slots_in, slots_out):
    with ExitStack() as ctx:
        def sb(name, shape, dt=F32):
            return ctx.enter_context(nc.sbuf_tensor(name, shape, dt))

        def whole(name, shape, dt=F32):
            return sb(name, shape, dt)[tuple(slice(None) for _ in shape)]

        def sem(name):
            return ctx.enter_context(nc.semaphore(name))

        consts = sb("consts", [P, CONST_COLS])

        def const(name):
            a, b = CONST[name]
            return consts[:, a:b]

        ident = const("ident")
        x = sb("x", [P, TILES, DIM])
        y = sb("y", [P, TILES, DIM])
        z = sb("z", [P, TILES, DIM])
        ctx_in = sb("ctx_in", [P, 2, TPU, DIM])
        wqkv = sb("wqkv", [P, LAYERS, 3, DIM])
        wrot = sb("wrot", [P, 2, DIM])
        wo = sb("wo", [P, LAYERS, DIM])
        cols = sb("cols", [P, 6])
        rows = sb("rows", [P, 2, DIM])
        bv = sb("bv", [P, DIM // 2])
        slopes = sb("slopes", [P, HEADS])
        gate_w = sb("gate_w", [P, EXPERTS])
        gate_b = sb("gate_b", [P, EXPERTS])
        w1 = sb("w1", [P, EXPERTS * HID])
        w2 = sb("w2", [P, EXPERTS * HID])
        pick16 = sb("pick16", [P, P], F16)
        alibi_qk = sb("alibi_qk", [P, HEADS, SEQ], F16)
        stats = sb("stats", [P, TPU, 6])
        mom = sb("mom", [P, TPU, 2])
        veps = sb("veps", [P, TPU])
        rstd = sb("rstd", [P, TPU])
        stats2 = sb("stats2", [P, TPU, 6])
        mom2 = sb("mom2", [P, TPU, 2])
        veps2 = sb("veps2", [P, TPU])
        rstd2 = sb("rstd2", [P, TPU])
        mhalf = sb("mhalf", [P, TPU])
        eps = sb("eps", [P, TPU])
        carrier = sb("carrier", [P, 1])
        xn = sb("xn", [P, TPU, DIM])
        xT = sb("xT", [P, COLS])
        cT = sb("cT", [P, COLS])
        rope_a = sb("rope_a", [P, 2 * COLS])
        rope_b = sb("rope_b", [P, 2 * COLS])
        qkT = sb("qkT", [P, 2, 2, COLS])
        km = sb("km", [P, 2, HEADS, COLS])
        vb = sb("vb", [P, 2, TPU, 2, PAIRS, 2 * HD + 2])
        mrow = sb("mrow", [P, TPU, HEADS])
        prob = sb("prob", [P, TPU, HEADS * SEQ])
        probT = sb("probT", [P, TPU, PAIRS, P])
        oT = sb("oT", [P, 2 * COLS])
        rc = sb("rc", [P, TPU * PAIRS, 2])
        on = sb("on", [P, TPU, DIM])
        hT = sb("hT", [P, COLS])
        zn = whole("zn", [P, 2, TPU, DIM])
        zT = whole("zT", [P, 2, COLS])
        xs = whole("xs", [P, RING, DIM])
        xsT = whole("xsT", [P, RING, P])
        hs = whole("hs", [P, RING, HID])
        hsT = whole("hsT", [P, RING, HID])
        ys = whole("ys", [P, RING, DIM])
        gstats = whole("gstats", [P, 2, TPU, 6])
        gmom = whole("gmom", [P, 2, TPU, 2])
        gveps = whole("gveps", [P, 2, TPU])
        grstd = whole("grstd", [P, 2, TPU])
        logits = whole("logits", [P, TILES, EXPERTS])
        best = whole("best", [P, TILES])
        tie = whole("tie", [P, TILES, EXPERTS])
        tie_best = whole("tie_best", [P, TILES])
        count = whole("count", [P, 2, TILES, EXPERTS])
        filled = whole("filled", [P, EXPERTS, TILES])
        used = whole("used", [P, EXPERTS])
        ends = whole("ends", [P, 2, EXPERTS])
        base = whole("base", [P, EXPERTS])
        place = whole("place", [P, 3, TILES, EXPERTS])
        slot_f = whole("slot_f", [P, TILES])
        passed = whole("passed", [P, SLOT_TILES, EXPERTS])
        expert_f = whole("expert_f", [P, SLOT_TILES])
        zero = sb("zero", [P, DIM])
        onehot = sb("onehot", [P, TILES, EXPERTS], BF16)
        before = sb("before", [P, P], BF16)
        ones = sb("ones", [P, P], BF16)
        slot = sb("slot", [P, TILES], I32)
        expert = sb("expert", [P, SLOT_TILES], I32)

        psum = ctx.enter_context(nc.psum_tensor("psum", [P, 8, 512], F32))
        s_ps = [psum[:, 2 * t:2 * t + 2, :].rearrange("p a c -> p (a c)") for t in range(TPU)]
        pv_ps = psum[:, 4, :]
        m0 = psum[:, 5, :]
        m1 = psum[:, 6, :]
        m2 = psum[:, 7, :]

        c_in, w_in, x_in, moe_in = sem("c_in"), sem("w_in"), sem("x_in"), sem("moe_in")
        ctx_sem = [sem("ctx_in0"), sem("ctx_in1")]
        ctx_used = sem("ctx_used")
        setup = sem("setup")
        setup_pool = sem("setup_pool")
        alibi_step = sem("alibi_step")
        d_stats, d_mom, d_xn = sem("d_stats"), sem("d_mom"), sem("d_xn")
        d_stats2, d_mom2, d_y = sem("d_stats2"), sem("d_mom2"), sem("d_y")
        d_max, d_sub = sem("d_max"), sem("d_sub")
        d_rope, d_qk, d_v = sem("d_rope"), sem("d_qk"), sem("d_v")
        d_rc, d_on, d_res = sem("d_rc"), sem("d_on"), sem("d_res")
        p_xT, p_qk, p_rot, p_v = sem("p_xT"), sem("p_qk"), sem("p_rot"), sem("p_v")
        p_s, p_pT, p_pv = sem("p_s"), sem("p_pT"), sem("p_pv")
        p_t1, p_t2, p_out = sem("p_t1"), sem("p_t2"), sem("p_out")
        a_xT, a_qk, a_exp, a_pT = sem("a_xT"), sem("a_qk"), sem("a_exp"), sem("a_pT")
        a_oT, a_hT, a_km = sem("a_oT"), sem("a_hT"), sem("a_km")
        g_veps, g_rstd, g_km, g_bias = sem("g_veps"), sem("g_rstd"), sem("g_km"), sem("g_bias")
        g_veps2, g_rstd2 = sem("g_veps2"), sem("g_rstd2")
        stored = sem("stored")
        zeroed = sem("zeroed")
        r_stats, r_mom, r_veps, r_rstd = sem("r_stats"), sem("r_mom"), sem("r_veps"), sem("r_rstd")
        r_zn, r_zT, r_zT_sb = sem("r_zn"), sem("r_zT"), sem("r_zT_sb")
        r_logits, r_biased, route, counted = sem("r_logits"), sem("r_biased"), sem("route"), sem("counted")
        routed, scattered, xy_sum = sem("routed"), sem("scattered"), sem("xy_sum")
        e_in = [sem(f"e_in{r}") for r in range(RING)]
        e_out = [sem(f"e_out{r}") for r in range(RING)]
        e_xT, e_xT_sb, e_up, e_gelu = sem("e_xT"), sem("e_xT_sb"), sem("e_up"), sem("e_gelu")
        e_hT, e_hT_sb, e_down, e_y = sem("e_hT"), sem("e_hT_sb"), sem("e_down"), sem("e_y")
        gathered = [sem(f"gathered{g}") for g in range(GROUPS)]
        summed = sem("summed")


        def unit(layer, u, least=None):
            least = u if least is None else least
            if least < 0:
                layer, u, least = layer - 1, u + UNITS, least + UNITS
            return Unit(layer, u, layer * UNITS + u, layer * UNITS + least) if 0 <= layer < LAYERS else None

        def pipeline(eng, step):
            for layer in range(LAYERS + 1):
                for u in range(4 if layer < LAYERS else 3):
                    step(*(unit(layer, u - k) for k in range(4)), u % 2)
                if layer < LAYERS:
                    with eng.Fori(2, UNITS // 2) as i:
                        for par in (0, 1):
                            step(*(unit(layer, 2 * i + (par - k), 4 + par - k) for k in range(4)), par)

        def gate_pipeline(eng, step):
            for s in range(4):
                step(s, s, s % 2)
            with eng.Fori(2, UNITS // 2) as i:
                for par in (0, 1):
                    step(2 * i + par, 4 + par, par)
            for s in range(UNITS, UNITS + 3):
                step(s, s, s % 2)

        def behind(s, least, lag, end):
            if least < lag or (isinstance(s, int) and s - lag >= end):
                return None
            return s - lag

        def expert_pipeline(eng, step, lag):
            for s in range(2 * RING):
                step(s, s, s % RING, s // RING)
            with eng.Fori(2, SLOT_TILES // RING) as lap:
                for r in range(RING):
                    step(RING * lap + r, 2 * RING + r, r, lap)
            for s in range(SLOT_TILES, SLOT_TILES + lag):
                step(s, s, s % RING, s // RING)

        def tok(par_t, b):
            return slice(par_t * P + b * SEQ, par_t * P + (b + 1) * SEQ)

        block = ctx.enter_context(nc.Block())

        @block.sync
        def _(sp):
            sp.dma_start(consts[:, :], ins["consts"]).then_inc(c_in, 16)
            xv = ins["x"].rearrange("(t r) s d -> (r s) t d", r=2)
            sp.dma_start(x[:, 0:4, :], xv[:, 0:4, :]).then_inc(x_in, 16)
            for dst, name in ((wqkv[:, :, :, :].rearrange("p a b c -> p (a b c)"), "wqkv"),
                              (wrot[:, :, :].rearrange("p a c -> p (a c)"), "wrot"), (cols[:, :], "cols"),
                              (rows[:, :, :].rearrange("p a c -> p (a c)"), "rows"), (slopes[:, :], "slopes"),
                              (wo[:, :, :].rearrange("p a c -> p (a c)"), "wo"), (bv[:, :], "bv"),
                              (gate_w[:, :], "gate_w"), (gate_b[:, :], "gate_b")):
                sp.dma_start(dst, ins[name]).then_inc(w_in, 16)
            sp.dma_start(x[:, 4:TILES, :], xv[:, 4:TILES, :]).then_inc(x_in, 16)
            sp.dma_start(w1[:, :], ins["w1"]).then_inc(moe_in, 16)
            sp.dma_start(w2[:, :], ins["w2"]).then_inc(moe_in, 16)
            cv = ins["ctx"].rearrange("(u t r) s d -> u (r s) t d", r=2, t=TPU)
            for u in (0, 1):
                sp.dma_start(ctx_in[:, u, :, :], cv[u]).then_inc(ctx_sem[u], 16)
            with sp.Fori(1, UNITS // 2) as i:
                for par in (0, 1):
                    sp.wait_ge(ctx_used, 2 * i + (par - 1))
                    sp.dma_start(ctx_in[:, par, :, :], cv[2 * i + par]).then_inc(ctx_sem[par], 16)

            sp.wait_ge(setup_pool, 3)
            sp.dma_start(slots_in.rearrange("(t p) d -> p t d", p=P),
                         zero[:, None, :].broadcast_to([P, SLOT_TILES, DIM])).then_inc(zeroed, 16)
            sp.wait_ge(scattered, 16 * TILES)

            def step(s, least, r, lap):
                j = behind(s, least, 0, SLOT_TILES)
                if j is not None:
                    if least >= RING:
                        sp.wait_ge(e_xT, j - RING + 1)
                    sp.dma_start(xs[:, r, :], slots_in[bass.ds(P * j, P), :]).then_inc(e_in[r], 16)
                j = behind(s, least, 3, SLOT_TILES)
                if j is not None:
                    sp.wait_ge(e_y, j + 1)
                    sp.dma_start(slots_out[bass.ds(P * j, P), :], ys[:, r, :]).then_inc(e_out[r], 16)

            expert_pipeline(sp, step, 3)
            ov = out.rearrange("(t r) s d -> (r s) t d", r=2)
            for g in range(GROUPS):
                part = slice(g * TILES // GROUPS, (g + 1) * TILES // GROUPS)
                sp.wait_ge(summed, g + 1)
                sp.dma_start(ov[:, part, :], z[:, part, :]).then_inc(stored, 16)
            sp.wait_ge(stored, 16 * GROUPS)

        @block.gpsimd
        def _(pool):
            nc.gpsimd.memset(mhalf[:, :], -0.5).then_inc(setup_pool, 1)
            nc.gpsimd.memset(eps[:, :], EPS).then_inc(setup_pool, 1)
            nc.gpsimd.memset(zero[:, :], 0.0).then_inc(setup_pool, 1)
            pool.wait_ge(setup_pool, 3)
            pool.wait_ge(c_in, 16)

            def keys_apart(F, par, heads):
                for h in heads:
                    if h == 0:
                        last = nc.gpsimd.tensor_tensor(km[:, par, 0, :], qkT[:, par, 1, :],
                                                       const("head_mask")[:, 0:1].broadcast_to([P, COLS]), ALU.mult)
                    else:
                        last = nc.gpsimd.tensor_scalar(km[:, par, h, :], qkT[:, par, 1, :],
                                                       const("head_mask")[:, h:h + 1], 1.0, ALU.mult, ALU.mult)
                return last

            def step(G, F, C, B, par):
                if G is not None:
                    n = G.n
                    pool.wait_ge(d_mom, 2 * n + 2)
                    nc.gpsimd.tensor_tensor(veps[:, :], mom[:, :, 1], eps[:, :], ALU.add).then_inc(g_veps, 1)
                    pool.wait_ge(g_veps, n + 1)
                    nc.gpsimd.tensor_tensor(rstd[:, :], veps[:, :], mhalf[:, :], ALU.pow).then_inc(g_rstd, 1)
                if F is not None:
                    f = F.n
                    pool.wait_ge(a_qk if F.layer else d_qk, f + 1 - (UNITS if F.layer else 0))
                    if F.least > 1:
                        pool.wait_ge(p_s, 2 * f - 2)
                    keys_apart(F, 1 - par, range(4))
                if G is not None and G.layer == 2:
                    m = G.u
                    pool.wait_ge(d_mom2, 2 * m + 2)
                    nc.gpsimd.tensor_tensor(veps2[:, :], mom2[:, :, 1], eps[:, :], ALU.add).then_inc(g_veps2, 1)
                    pool.wait_ge(g_veps2, m + 1)
                    nc.gpsimd.tensor_tensor(rstd2[:, :], veps2[:, :], mhalf[:, :], ALU.pow).then_inc(g_rstd2, 1)
                if F is not None:
                    keys_apart(F, 1 - par, range(4, POOL_HEADS)).then_inc(g_km, 1)
                if G is not None and G.layer < 2:
                    pool.wait_ge(d_xn, n + 1)
                    here = x[:, bass.ds(TPU * G.u, TPU), :]
                    nc.gpsimd.tensor_tensor(here, here, rows[:, G.layer, None, :].broadcast_to([P, TPU, DIM]),
                                            ALU.add).then_inc(g_bias, 1)

            pipeline(pool, step)

            def gate_step(s, least, par):
                u = behind(s, least, 0, UNITS)
                if u is not None:
                    pool.wait_ge(r_mom, u + 1)
                    nc.gpsimd.tensor_tensor(gveps[:, par, :], gmom[:, par, :, 1], eps[:, :], ALU.add).then_inc(r_veps, 1)
                    pool.wait_ge(r_veps, u + 1)
                    nc.gpsimd.tensor_tensor(grstd[:, par, :], gveps[:, par, :], mhalf[:, :], ALU.pow).then_inc(r_rstd, 1)

            gate_pipeline(pool, gate_step)
            pool.wait_ge(zeroed, 16)
            pool.wait_ge(routed, 1)
            for t in range(TILES):
                nc.gpsimd.indirect_dma_start(out=slots_in, out_offset=bass.IndirectOffsetOnAxis(ap=slot[:, t:t + 1], axis=0),
                                             in_=z[:, t, :], in_offset=None).then_inc(scattered, 16)
            for r in range(RING):
                pool.wait_ge(e_out[r], 16 * SLOT_TILES // RING)
            for g in range(GROUPS):
                for t in range(g * TILES // GROUPS, (g + 1) * TILES // GROUPS):
                    nc.gpsimd.indirect_dma_start(out=z[:, t, :], out_offset=None, in_=slots_out,
                                                 in_offset=bass.IndirectOffsetOnAxis(ap=slot[:, t:t + 1], axis=0),
                                                 ).then_inc(gathered[g], 16)

        @block.scalar
        def _(act):
            def transposed(U, t):
                n = U.n
                act.wait_ge(p_pT, 2 * n + t + 1)
                nc.scalar.activation(probT[:, t, :, :].rearrange("p a q -> p (a q)"), s_ps[t], ACT.Copy).then_inc(a_pT, 1)

            def exponentials(U, t):
                n = U.n
                act.wait_ge(d_sub, 2 * n + t + 1)
                nc.scalar.activation(prob[:, t, :], prob[:, t, :], ACT.Exp, scale=SCALE).then_inc(a_exp, 1)

            def keys_apart(F, par, heads):
                for h in heads:
                    last = nc.scalar.activation(km[:, par, h, :], qkT[:, par, 1, :], ACT.Copy,
                                                scale=const("head_mask")[:, h:h + 1])
                return last

            def step(G, F, C, B, par):
                fpar = 1 - par
                if F is not None:
                    f = F.n
                    if F.layer:
                        act.wait_ge(p_qk, f + 1)
                        act.wait_ge(p_s, 2 * f - 2)
                        act.wait_ge(g_km, f - 1)
                        if F.layer == 1:
                            for i in range(2):
                                last = nc.scalar.activation(qkT[:, fpar, i, :], m1[:, i * COLS:(i + 1) * COLS],
                                                            ACT.Identity, bias=cols[:, i:i + 1])
                        else:
                            last = nc.scalar.activation(qkT[:, fpar, :, :].rearrange("p a c -> p (a c)"), m1, ACT.Copy)
                        last.then_inc(a_qk, 1)
                if B is not None:
                    transposed(B, 1)
                if F is not None:
                    act.wait_ge(a_qk if F.layer else d_qk, f + 1 - (UNITS if F.layer else 0))
                    if F.least > 1:
                        act.wait_ge(p_s, 2 * f - 2)
                    keys_apart(F, fpar, range(POOL_HEADS, HEADS - 2))
                if B is not None:
                    b_ = B.n
                    act.wait_ge(p_pv, 2 * b_ + 2)
                    if B.least:
                        act.wait_ge(p_t1, b_)
                    nc.scalar.activation(oT[:, :], pv_ps, ACT.Copy).then_inc(a_oT, 1)
                if F is not None:
                    keys_apart(F, fpar, range(HEADS - 2, HEADS)).then_inc(a_km, 1)
                if C is not None:
                    exponentials(C, 0)
                if B is not None:
                    act.wait_ge(p_t2, b_ + 1)
                    if B.least:
                        act.wait_ge(p_out, b_)
                    nc.scalar.activation(hT[:, :], m2[:, 0:COLS], ACT.Copy).then_inc(a_hT, 1)
                if C is not None:
                    transposed(C, 0)
                if G is not None:
                    n = G.n
                    act.wait_ge(p_xT, n + 1)
                    if G.least:
                        act.wait_ge(p_v, n)
                    if G.layer == 1:
                        nc.scalar.activation(cT[:, :], m1[:, COLS:2 * COLS], ACT.Copy)
                    if G.layer == 2:
                        nc.scalar.activation(xT[:, :], m1[:, 0:COLS], ACT.Identity, bias=cols[:, 3:4],
                                             scale=cols[:, 2:3]).then_inc(a_xT, 1)
                    else:
                        nc.scalar.activation(xT[:, :], m1[:, 0:COLS], ACT.Copy).then_inc(a_xT, 1)
                if C is not None:
                    exponentials(C, 1)

            act.wait_ge(c_in, 16)
            act.wait_ge(w_in, 16 * WEIGHTS)
            pipeline(act, step)

            def gate_step(s, least, par):
                u = behind(s, least, 2, UNITS)
                if u is not None:
                    act.wait_ge(r_zn, u + 1)
                    nc.scalar.activation(z[:, bass.ds(TPU * u, TPU), :], zn[:, par, :, :], ACT.Copy)
                    act.wait_ge(r_zT, u + 1)
                    nc.scalar.activation(zT[:, par, :], (m0, m1)[par][:, 0:COLS], ACT.Identity, bias=cols[:, 5:6],
                                         scale=cols[:, 4:5]).then_inc(r_zT_sb, 1)

            gate_pipeline(act, gate_step)

            def expert_step(s, least, r, lap):
                j = behind(s, least, 0, SLOT_TILES)
                if j is not None:
                    act.wait_ge(e_xT, j + 1)
                    nc.scalar.activation(xsT[:, r, :], psum[:, 6, 0:P], ACT.Identity, bias=cols[:, 5:6],
                                         scale=cols[:, 4:5]).then_inc(e_xT_sb, 1)
                j = behind(s, least, 1, SLOT_TILES)
                if j is not None:
                    q = (r - 1) % RING
                    act.wait_ge(e_up, j + 1)
                    nc.scalar.activation(hs[:, q, :], psum[:, q, :], ACT.Gelu_apprx_tanh).then_inc(e_gelu, 1)

            expert_pipeline(act, expert_step, 1)

        @block.vector
        def _(dve):
            nc.vector.memset(vb[:, :, :, :, :, :], 0.0).then_inc(alibi_step, 1)
            nc.vector.memset(pv_ps, 0.0)
            dve.wait_ge(alibi_step, 1)
            nc.vector.memset(vb[0:64, :, :, :, :, 16:17], 1.0)
            nc.vector.memset(vb[64:128, :, :, :, :, 17:18], 1.0).then_inc(setup, 1)
            dve.wait_ge(c_in, 16)
            nc.vector.tensor_copy(pick16[:, :], const("pick")).then_inc(setup, 1)
            dve.wait_ge(w_in, 16 * WEIGHTS)
            exact = prob[:, 0, :].rearrange("p (h s) -> p h s", h=HEADS)
            nc.vector.tensor_tensor(exact, const("dist_qk")[:, None, :].broadcast_to([P, HEADS, SEQ]),
                                    slopes[:, :, None].broadcast_to([P, HEADS, SEQ]), ALU.mult).then_inc(alibi_step, 1)
            dve.wait_ge(alibi_step, 2)
            nc.vector.tensor_copy(alibi_qk[:, :, :], exact).then_inc(alibi_step, 1)
            dve.wait_ge(alibi_step, 3)
            nc.vector.tensor_tensor(alibi_qk[64:128, :, :], exact[64:128, :, :], alibi_qk[64:128, :, :],
                                    ALU.subtract).then_inc(alibi_step, 1)
            dve.wait_ge(alibi_step, 4)

            def maxima(C, t):
                dve.wait_ge(p_s, 2 * C.n + t + 1)
                nc.vector.tensor_reduce(mrow[:, t, :], s_ps[t].rearrange("p (h s) -> p h s", h=HEADS), AX.X,
                                        ALU.max).then_inc(d_max, 1)

            def subtract(C, t):
                dve.wait_ge(d_max, 2 * C.n + t + 1)
                nc.vector.tensor_tensor(prob[:, t, :].rearrange("p (h s) -> p h s", h=HEADS),
                                        s_ps[t].rearrange("p (h s) -> p h s", h=HEADS),
                                        mrow[:, t, :, None].broadcast_to([P, HEADS, SEQ]), ALU.subtract).then_inc(d_sub, 1)

            def step(G, F, C, B, par):
                fpar = 1 - par
                if G is not None:
                    n = G.n
                    if G.layer == 0:
                        dve.wait_ge(x_in, 16 if G.least < 2 else 32)
                    else:
                        dve.wait_ge(d_res, n - UNITS + 1)
                    if G.least:
                        dve.wait_ge(g_veps, n)
                        dve.wait_ge(p_xT, n)
                        nc.vector.memset(carrier[:, :], 0.0)
                    for t in range(TPU):
                        nc.vector.bn_stats(stats[:, t, :], x[:, TPU * G.u + t, :]).then_inc(d_stats, 1)
                    dve.wait_ge(d_stats, 2 * n + 2)
                    nc.vector.memset(carrier[:, :], 0.0)
                    for t in range(TPU):
                        nc.vector.bn_aggr(mom[:, t, :], stats[:, t, :]).then_inc(d_mom, 1)
                if F is not None and F.layer == 0:
                    f = F.n
                    dve.wait_ge(p_qk, f + 1)
                    tab = lambda name: const(name)[:, None, :].broadcast_to([P, 2 * COLS // SEQ, SEQ])
                    blocks = lambda ap: ap.rearrange("p (b s) -> p b s", s=SEQ)
                    if F.least:
                        dve.wait_ge(d_qk, f)
                    nc.vector.tensor_tensor(blocks(rope_a[:, :]), blocks(m1), tab("cos"), ALU.mult).then_inc(d_rope, 1)
                    dve.wait_ge(p_rot, f + 1)
                    nc.vector.tensor_tensor(blocks(rope_b[:, :]), blocks(m0), tab("sin"), ALU.mult).then_inc(d_rope, 1)
                    dve.wait_ge(d_rope, 2 * f + 2)
                    if F.least > 1:
                        dve.wait_ge(p_s, 2 * f - 2)
                        dve.wait_ge(g_km, f - 1)
                        dve.wait_ge(a_km, f - 1)
                    nc.vector.tensor_tensor(qkT[:, fpar, :, :].rearrange("p a c -> p (a c)"), rope_a[:, :], rope_b[:, :],
                                            ALU.add).then_inc(d_qk, 1)
                if G is not None:
                    dve.wait_ge(g_rstd, n + 1)
                    dst = (lambda t: y[:, TPU * G.u + t, :]) if G.layer == 2 else (lambda t: xn[:, t, :])
                    for t in range(TPU):
                        last = nc.vector.tensor_scalar(dst(t), x[:, TPU * G.u + t, :], mom[:, t, 0:1], rstd[:, t:t + 1],
                                                       ALU.subtract, ALU.mult)
                    if G.layer != 2:
                        last.then_inc(d_xn, 1)
                    else:
                        m = G.u
                        last.then_inc(d_y, 1)
                        dve.wait_ge(d_y, m + 1)
                        nc.vector.memset(carrier[:, :], 0.0)
                        for t in range(TPU):
                            nc.vector.bn_stats(stats2[:, t, :], y[:, TPU * G.u + t, :]).then_inc(d_stats2, 1)
                        dve.wait_ge(d_stats2, 2 * m + 2)
                        nc.vector.memset(carrier[:, :], 0.0)
                        for t in range(TPU):
                            nc.vector.bn_aggr(mom2[:, t, :], stats2[:, t, :]).then_inc(d_mom2, 1)
                if C is not None:
                    maxima(C, 0)
                    subtract(C, 0)
                if G is not None and G.layer == 2:
                    dve.wait_ge(g_rstd2, m + 1)
                    for t in range(TPU):
                        last = nc.vector.tensor_scalar(xn[:, t, :], y[:, TPU * G.u + t, :], mom2[:, t, 0:1],
                                                       rstd2[:, t:t + 1], ALU.subtract, ALU.mult)
                    last.then_inc(d_xn, 1)
                if B is not None:
                    b_ = B.n
                    dve.wait_ge(p_t1, b_ + 1)
                    t1 = m2.rearrange("p (g w) -> p g w", w=32)
                    nc.vector.reciprocal(rc[:, :, :], t1[:, :, 2 * HD:2 * HD + 2]).then_inc(d_rc, 1)
                    dve.wait_ge(d_rc, b_ + 1)
                    if B.least:
                        dve.wait_ge(p_t2, b_)
                    nc.vector.tensor_tensor(on[:, :, :].rearrange("p t (k o d) -> p (t k) o d", o=2, d=HD),
                                            t1[:, :, 0:2 * HD].rearrange("p g (o d) -> p g o d", o=2),
                                            rc[:, :, :, None].broadcast_to([P, TPU * PAIRS, 2, HD]), ALU.mult).then_inc(d_on, 1)
                if F is not None:
                    f = F.n
                    dve.wait_ge(p_v, f + 1)
                    if F.least > 1:
                        dve.wait_ge(p_pv, 2 * f - 2)
                    for odd in range(2):
                        part = slice(64 * odd, 64 * odd + 64)
                        src = m0[part, 0:COLS].rearrange("p (a k d) -> p a k d", k=PAIRS, d=HD)
                        dst = vb[part, fpar, :, :, :, HD * odd:HD * odd + HD].rearrange("p t b k d -> p (t b) k d")
                        if F.layer == 1:
                            bias = bv[part, :].rearrange("p (k d) -> p k d", d=HD)[:, None, :, :]
                            last = nc.vector.tensor_tensor(dst, src, bias.broadcast_to([64, 2 * TPU, PAIRS, HD]), ALU.add)
                        else:
                            last = nc.vector.tensor_copy(dst, src)
                    last.then_inc(d_v, 1)
                if C is not None:
                    maxima(C, 1)
                    subtract(C, 1)
                if B is not None:
                    dve.wait_ge(p_out, b_ + 1)
                    if B.layer < 2:
                        dve.wait_ge(g_bias, b_ + 1)
                    here = (x if B.layer < 2 else y)[:, bass.ds(TPU * B.u, TPU), :]
                    nc.vector.tensor_tensor(here, here, m2[:, COLS:2 * COLS].rearrange("p (t d) -> p t d", t=TPU),
                                            ALU.add).then_inc(d_res, 1)

            pipeline(dve, step)

            nc.vector.tensor_copy(before[:, :], const("before"))
            nc.vector.memset(ones[:, :], 1.0)
            dve.wait_ge(d_res, LAYERS * UNITS)
            nc.vector.memset(carrier[:, :], 0.0)

            def gate_step(s, least, par):
                u = behind(s, least, 0, UNITS)
                if u is not None:
                    for t in range(TPU):
                        nc.vector.bn_stats(gstats[:, par, t, :], y[:, TPU * u + t, :]).then_inc(r_stats, 1)
                    dve.wait_ge(r_stats, 2 * u + 2)
                    if least >= 2:
                        dve.wait_ge(r_zn, u - 1)
                    nc.vector.memset(carrier[:, :], 0.0)
                    for t in range(TPU):
                        last = nc.vector.bn_aggr(gmom[:, par, t, :], gstats[:, par, t, :])
                    last.then_inc(r_mom, 1)
                u = behind(s, least, 1, UNITS)
                if u is not None:
                    dve.wait_ge(r_rstd, u + 1)
                    if least >= 3:
                        dve.wait_ge(r_zT_sb, u - 1)
                    for t in range(TPU):
                        last = nc.vector.tensor_scalar(zn[:, 1 - par, t, :], y[:, TPU * u + t, :],
                                                       gmom[:, 1 - par, t, 0:1], grstd[:, 1 - par, t:t + 1],
                                                       ALU.subtract, ALU.mult)
                    last.then_inc(r_zn, 1)
                u = behind(s, least, 3, UNITS)
                if u is not None:
                    dve.wait_ge(r_logits, u + 1)
                    nc.vector.tensor_tensor(logits[:, bass.ds(TPU * u, TPU), :],
                                            (m0, m1)[1 - par][:, COLS:COLS + TPU * EXPERTS].rearrange("p (t e) -> p t e", t=TPU),
                                            gate_b[:, None, :].broadcast_to([P, TPU, EXPERTS]), ALU.add).then_inc(r_biased, 1)

            gate_pipeline(dve, gate_step)

            TE = [P, TILES, EXPERTS]
            by_tile = lambda a: a[:, :, None].broadcast_to(TE)
            by_expert = lambda a: a[:, None, :].broadcast_to(TE)
            dve.wait_ge(r_biased, UNITS)
            nc.vector.tensor_reduce(best, logits, AX.X, ALU.max).then_inc(route, 1)
            dve.wait_ge(route, 1)
            nc.vector.tensor_tensor(tie, logits, by_tile(best), ALU.is_ge).then_inc(route, 1)
            dve.wait_ge(route, 2)
            nc.vector.tensor_tensor(tie, tie, by_expert(const("first")), ALU.mult).then_inc(route, 1)
            dve.wait_ge(route, 3)
            nc.vector.tensor_reduce(tie_best, tie, AX.X, ALU.max).then_inc(route, 1)
            dve.wait_ge(route, 4)
            nc.vector.tensor_tensor(onehot[:, :, :], tie, by_tile(tie_best), ALU.is_equal).then_inc(route, 1)
            in_tile = psum[:, 0, 0:TILES * EXPERTS].rearrange("p (t e) -> p t e", t=TILES)
            total = psum[:, 1, 0:TILES * EXPERTS].rearrange("p (t e) -> p t e", t=TILES)
            dve.wait_ge(counted, 2)
            nc.vector.tensor_copy(count[:, 0, :, :], total).then_inc(route, 1)
            done, now, shift = 6, 0, 1
            while shift < TILES:
                dve.wait_ge(route, done)
                nc.vector.tensor_copy(count[:, 1 - now, 0:shift, :], count[:, now, 0:shift, :])
                nc.vector.tensor_tensor(count[:, 1 - now, shift:TILES, :], count[:, now, shift:TILES, :],
                                        count[:, now, 0:TILES - shift, :], ALU.add).then_inc(route, 1)
                done, now, shift = done + 1, 1 - now, 2 * shift
            upto_tile = count[:, now, :, :]
            dve.wait_ge(route, done)
            nc.vector.tensor_tensor(filled, upto_tile[:, TILES - 1, :, None].broadcast_to([P, EXPERTS, TILES]),
                                    const("slot128")[:, None, :].broadcast_to([P, EXPERTS, TILES]),
                                    ALU.is_gt).then_inc(route, 1)
            nc.vector.tensor_tensor(place[:, 0, :, :], in_tile, upto_tile, ALU.add)
            dve.wait_ge(route, done + 1)
            nc.vector.tensor_reduce(used, filled, AX.X, ALU.add).then_inc(route, 1)
            dve.wait_ge(route, done + 2)
            nc.vector.tensor_copy(ends[:, 0, :], used).then_inc(route, 1)
            nc.vector.tensor_tensor(place[:, 1, :, :], place[:, 0, :, :], total, ALU.subtract)
            done, now, shift = done + 3, 0, 1
            while shift < EXPERTS:
                dve.wait_ge(route, done)
                nc.vector.tensor_copy(ends[:, 1 - now, 0:shift], ends[:, now, 0:shift])
                nc.vector.tensor_tensor(ends[:, 1 - now, shift:EXPERTS], ends[:, now, shift:EXPERTS],
                                        ends[:, now, 0:EXPERTS - shift], ALU.add).then_inc(route, 1)
                done, now, shift = done + 1, 1 - now, 2 * shift
            last_tile = ends[:, now, :]
            dve.wait_ge(route, done)
            nc.vector.tensor_tensor(base, last_tile, used, ALU.subtract).then_inc(route, 1)
            nc.vector.tensor_tensor(passed, const("tile_no")[:, :, None].broadcast_to([P, SLOT_TILES, EXPERTS]),
                                    last_tile[:, None, :].broadcast_to([P, SLOT_TILES, EXPERTS]), ALU.is_ge).then_inc(route, 1)
            dve.wait_ge(route, done + 2)
            nc.vector.scalar_tensor_tensor(out=place[:, 2, :, :], in0=by_expert(base), scalar=float(P),
                                           in1=place[:, 1, :, :], op0=ALU.mult, op1=ALU.add).then_inc(route, 1)
            nc.vector.tensor_reduce(expert_f, passed, AX.X, ALU.add).then_inc(route, 1)
            dve.wait_ge(route, done + 4)
            nc.vector.tensor_tensor(place[:, 0, :, :], place[:, 2, :, :], onehot[:, :, :], ALU.mult).then_inc(route, 1)
            nc.vector.tensor_scalar(expert[:, :], expert_f, float(EXPERTS - 1), float(HID), ALU.min, ALU.mult)
            dve.wait_ge(route, done + 5)
            nc.vector.tensor_reduce(slot_f, place[:, 0, :, :], AX.X, ALU.add).then_inc(route, 1)
            dve.wait_ge(route, done + 6)
            nc.vector.tensor_scalar(slot[:, :], slot_f, float(SLOT_TILES * P - 1), None, ALU.min).then_inc(routed, 1)
            nc.vector.tensor_tensor(x[:, :, :], x[:, :, :], y[:, :, :], ALU.add).then_inc(xy_sum, 1)

            def expert_step(s, least, r, lap):
                j = behind(s, least, 2, SLOT_TILES)
                if j is not None:
                    q = (r - 2) % RING
                    dve.wait_ge(e_hT, j + 1)
                    nc.vector.tensor_copy(hsT[:, q, :], psum[:, q, :]).then_inc(e_hT_sb, 1)
                    dve.wait_ge(e_down, j + 1)
                    if least - 2 >= RING:
                        dve.wait_ge(e_out[q], 16 * (lap + (r - 2) // RING))
                    nc.vector.tensor_copy(ys[:, q, :], psum[:, 3 + q, P:2 * P]).then_inc(e_y, 1)

            expert_pipeline(dve, expert_step, 2)
            dve.wait_ge(xy_sum, 1)
            for g in range(GROUPS):
                part = slice(g * TILES // GROUPS, (g + 1) * TILES // GROUPS)
                dve.wait_ge(gathered[g], 16 * TILES // GROUPS)
                nc.vector.tensor_tensor(z[:, part, :], z[:, part, :], x[:, part, :], ALU.add).then_inc(summed, 1)

        @block.tensor
        def _(pe):
            mm = nc.tensor.matmul

            def scores(C, t, par):
                n = C.n
                if t == 0:
                    pe.wait_ge(g_km, n + 1)
                    pe.wait_ge(a_km, n + 1)
                if C.least:
                    pe.wait_ge(a_pT, 2 * n + (t - 1))
                if C.layer == 0:
                    for half in range(2):
                        mm(s_ps[t][:, half * 512:(half + 1) * 512], pick16[:, :],
                           alibi_qk[:, half * HALF:(half + 1) * HALF, :], start=True, stop=False, skip_group_check=True)
                for half in range(2):
                    for b in range(2):
                        last = mm(s_ps[t][64 * b:64 * b + 64, half * 512:(half + 1) * 512], qkT[:, par, 0, tok(t, b)],
                                  km[:, par, half * HALF:(half + 1) * HALF, tok(t, b)], start=C.layer != 0, stop=True,
                                  skip_group_check=True)
                last.then_inc(p_s, 1)

            def transposes(U, t):
                pe.wait_ge(a_exp, 2 * U.n + t + 1)
                for k in range(PAIRS):
                    last = mm(s_ps[t][:, k * P:(k + 1) * P], prob[:, t, k * P:(k + 1) * P], ident, is_transpose=True,
                              start=True, stop=True)
                last.then_inc(p_pT, 1)

            def values(U, t, par):
                n = U.n
                pe.wait_ge(a_pT, 2 * n + t + 1)
                if t == 0:
                    pe.wait_ge(d_v, n + 1)
                    if U.least:
                        pe.wait_ge(a_oT, n)
                for k in range(PAIRS):
                    for b in range(2):
                        c, g = k % 4, 4 * t + 2 * (k // 4) + b
                        last = mm(pv_ps[32 * c:32 * c + 2 * HD + 2, g * SEQ:(g + 1) * SEQ], vb[:, par, t, b, k, :],
                                  probT[:, t, k, b * SEQ:(b + 1) * SEQ], start=True, stop=True, tile_position=(0, 32 * c))
                last.then_inc(p_pv, 1)

            def step(G, F, C, B, par):
                fpar = 1 - par
                if F is not None:
                    f = F.n
                    pe.wait_ge(a_xT, f + 1)
                    for i in range(2):
                        last = mm(m1[:, i * COLS:(i + 1) * COLS], wqkv[:, F.layer, i, :],
                                  cT[:, :] if i and F.layer == 1 else xT[:, :], start=True, stop=True)
                    last.then_inc(p_qk, 1)
                    if F.least:
                        pe.wait_ge(d_v, f)
                    if F.layer == 0:
                        for i in range(2):
                            last = mm(m0[:, i * COLS:(i + 1) * COLS], wrot[:, i, :], xT[:, :], start=True, stop=True)
                        last.then_inc(p_rot, 1)
                if B is not None:
                    transposes(B, 1)
                if C is not None:
                    scores(C, 0, par)
                if B is not None:
                    values(B, 1, fpar)
                if F is not None:
                    if F.layer == 0:
                        pe.wait_ge(d_rope, 2 * f + 2)
                    for t in range(TPU):
                        for b in range(2):
                            for odd in range(2):
                                last = mm(m0[64 * odd:64 * odd + 64, (2 * t + b) * 64:(2 * t + b + 1) * 64],
                                          (cT if F.layer == 1 else xT)[:, tok(t, b)],
                                          wqkv[:, F.layer, 2, odd * 64:(odd + 1) * 64], start=True, stop=True)
                    last.then_inc(p_v, 1)
                if B is not None:
                    b_ = B.n
                    pe.wait_ge(a_oT, b_ + 1)
                    if B.least:
                        pe.wait_ge(d_res, b_)
                    for k in range(2 * TPU):
                        last = mm(m2[:, k * P:(k + 1) * P], oT[:, k * P:(k + 1) * P], ident, is_transpose=True,
                                  start=True, stop=True)
                    last.then_inc(p_t1, 1)
                if C is not None:
                    scores(C, 1, par)
                if B is not None:
                    pe.wait_ge(d_on, b_ + 1)
                    for t in range(TPU):
                        last = mm(m2[:, t * P:(t + 1) * P], on[:, t, :], ident, is_transpose=True, start=True, stop=True)
                    last.then_inc(p_t2, 1)
                if C is not None:
                    transposes(C, 0)
                if G is not None:
                    n = G.n
                    pe.wait_ge(d_xn, n + 1)
                    if F is not None:
                        if F.layer == 0:
                            pe.wait_ge(d_rope, 2 * f + 2)
                        else:
                            pe.wait_ge(a_qk, f - UNITS + 1)
                    if G.layer == 1:
                        pe.wait_ge(ctx_sem[par], 8 * (G.u - par) + 16)
                        for t in range(TPU):
                            last = mm(m1[:, COLS + t * P:COLS + (t + 1) * P], ctx_in[:, par, t, :], ident,
                                      is_transpose=True, start=True, stop=True)
                        last.then_inc(ctx_used, 1)
                    for t in range(TPU):
                        last = mm(m1[:, t * P:(t + 1) * P], xn[:, t, :], ident, is_transpose=True, start=True, stop=True)
                    last.then_inc(p_xT, 1)
                if B is not None:
                    pe.wait_ge(a_hT, b_ + 1)
                    for t in range(TPU):
                        last = mm(m2[:, COLS + t * P:COLS + (t + 1) * P], hT[:, t * P:(t + 1) * P], wo[:, B.layer, :],
                                  start=True, stop=True)
                    last.then_inc(p_out, 1)
                if C is not None:
                    values(C, 0, par)

            pe.wait_ge(c_in, 16)
            pe.wait_ge(w_in, 16 * WEIGHTS)
            pe.wait_ge(setup, 2)
            pe.wait_ge(alibi_step, 4)
            pipeline(pe, step)

            def gate_step(s, least, par):
                u = behind(s, least, 3, UNITS)
                if u is not None:
                    bank = (m0, m1)[1 - par]
                    pe.wait_ge(r_zT_sb, u + 1)
                    for t in range(TPU):
                        last = mm(bank[:, COLS + t * EXPERTS:COLS + (t + 1) * EXPERTS], zT[:, 1 - par, t * P:(t + 1) * P],
                                  gate_w[:, :], start=True, stop=True)
                    last.then_inc(r_logits, 1)
                u = behind(s, least, 2, UNITS)
                if u is not None:
                    pe.wait_ge(r_zn, u + 1)
                    if least >= 4:
                        pe.wait_ge(r_biased, u - 1)
                    for t in range(TPU):
                        last = mm((m0, m1)[par][:, t * P:(t + 1) * P], zn[:, par, t, :], ident, is_transpose=True,
                                  start=True, stop=True)
                    last.then_inc(r_zT, 1)

            gate_pipeline(pe, gate_step)
            pe.wait_ge(route, 5)
            for k, rows_used in enumerate((before, ones)):
                mm(psum[:, k, 0:TILES * EXPERTS], rows_used[:, :], onehot[:, :, :], start=True, stop=True).then_inc(counted, 1)

            def weight_column(j):
                return pe.value_load(expert[0:1, bass.ds(j, 1)], min_val=0, max_val=(EXPERTS - 1) * HID)

            def expert_step(s, least, r, lap):
                j = behind(s, least, 2, SLOT_TILES)
                q = (r - 2) % RING
                if j is not None:
                    pe.wait_ge(e_gelu, j + 1)
                    for c in range(CHUNKS):
                        last = mm(psum[:, q, c * P:(c + 1) * P], hs[:, q, c * P:(c + 1) * P], ident, is_transpose=True,
                                  start=True, stop=True)
                    last.then_inc(e_hT, 1)
                i = behind(s, least, 1, SLOT_TILES)
                if i is not None:
                    k = (r - 1) % RING
                    col = weight_column(i)
                    pe.wait_ge(e_xT_sb, i + 1)
                    if least - 1 >= RING:
                        pe.wait_ge(e_hT_sb, i - RING + 1)
                    mm(psum[:, k, :], xsT[:, k, :], w1[:, bass.ds(col, HID)], start=True, stop=True).then_inc(e_up, 1)
                i = behind(s, least, 0, SLOT_TILES)
                if i is not None:
                    pe.wait_ge(e_in[r], 16 * (lap + 1))
                    mm(psum[:, 6, 0:P], xs[:, r, :], ident, is_transpose=True, start=True, stop=True).then_inc(e_xT, 1)
                if j is not None:
                    col = weight_column(j)
                    pe.wait_ge(e_hT_sb, j + 1)
                    if least - 2 >= RING:
                        pe.wait_ge(e_y, j - RING + 1)
                    for c in range(CHUNKS):
                        last = mm(psum[:, 3 + q, P:2 * P], hsT[:, q, c * P:(c + 1) * P], w2[:, bass.ds(col + c * P, P)],
                                  start=c == 0, stop=c == CHUNKS - 1)
                    last.then_inc(e_down, 1)

            pe.wait_ge(routed, 1)
            pe.wait_ge(moe_in, 32)
            expert_pipeline(pe, expert_step, 2)


def constants(np):
    c = np.zeros((P, CONST_COLS), np.float32)

    def put(name, a):
        lo, hi = CONST[name]
        c[:, lo:hi] = a
    p = np.arange(P)
    put("ident", np.eye(P))
    put("pick", np.tile(np.eye(64), (2, 2)))
    put("head_mask", p[:, None] // HD == np.arange(HEADS))
    q = np.arange(SEQ)
    dist = np.minimum(q[None, :] - q[:, None], 0) * (8.0 / SCALE)
    put("dist_qk", np.tile(dist, (2, 1)))
    inv = (1.0 / 10000.0 ** (np.arange(0, HD, 2, dtype=np.float32) / HD)).astype(np.float32)
    ang = (q.astype(np.float32)[:, None] * inv[None, :]).astype(np.float32)
    put("cos", np.cos(ang).T[p % 4])
    put("sin", np.sin(ang).T[p % 4] * np.where(p % HD < 4, -1.0, 1.0)[:, None])
    put("before", p[:, None] < p[None, :])
    put("first", np.broadcast_to(EXPERTS - np.arange(EXPERTS), (P, EXPERTS)))
    put("slot128", np.broadcast_to(P * np.arange(TILES), (P, TILES)))
    put("tile_no", np.broadcast_to(np.arange(SLOT_TILES), (P, SLOT_TILES)))
    return c


def kernel(**inputs):
    import numpy as np
    import concourse.bacc as bacc
    from concourse.bass_utils import run_bass_kernel_spmd

    a = {k: np.asarray(v) for k, v in inputs.items()}

    qkv = a["L0_attn_qkv_w"].T
    parted = np.arange(DIM).reshape(PAIRS, 2, HD).transpose(1, 0, 2).reshape(-1)
    by_parted = lambda w: w[:, parted]
    rotated = np.arange(DIM) // HD * HD + (np.arange(DIM) + HD // 2) % HD
    every = lambda v: np.broadcast_to(v, (P, v.shape[-1]))
    arrays = {
        "consts": constants(np),
        "x": a["x"], "ctx": a["ctx_1024"],
        "wqkv": np.concatenate([qkv[:, :2 * DIM], by_parted(qkv[:, 2 * DIM:]),
                                a["L0_xattn_Wq"].T, a["L0_xattn_Wk"].T, by_parted(a["L0_xattn_Wv"].T),
                                a["L0_ffn_w_qkv"][:, :2 * DIM], by_parted(a["L0_ffn_w_qkv"][:, 2 * DIM:])], 1),
        "wrot": np.concatenate([qkv[:, rotated], qkv[:, DIM + rotated]], 1),
        "wo": np.concatenate([a["L0_attn_proj_w"].T, a["L0_xattn_Wo"].T, a["L0_ffn_w_proj"]], 1),
        "bv": np.repeat(a["L0_xattn_bv"][parted].reshape(2, 1, DIM // 2), 64, 1).reshape(P, DIM // 2),
        "cols": np.stack([a["L0_xattn_bq"], a["L0_xattn_bk"], a["L0_ffn_ln1_w"], a["L0_ffn_ln1_b"],
                          a["L0_ffn_ln2_w"], a["L0_ffn_ln2_b"]], 1),
        "rows": np.concatenate([every(a[k]) for k in ("L0_attn_proj_b", "L0_xattn_bo")], 1),
        "slopes": every(a["L0_attn_slopes"]),
        "gate_w": a["L0_ffn_gate_w"], "gate_b": every(a["L0_ffn_gate_b"]),
        "w1": a["L0_ffn_w1"].transpose(1, 0, 2).reshape(P, EXPERTS * HID),
        "w2": a["L0_ffn_w2"].reshape(EXPERTS, CHUNKS, P, DIM).transpose(2, 0, 1, 3).reshape(P, EXPERTS * HID),
    }
    arrays = {k: np.ascontiguousarray(v) for k, v in arrays.items()}
    nc = bacc.Bacc("TRN2", target_bir_lowering=False, num_devices=1)
    ins = {k: nc.dram_tensor(f"in_{k}", v.shape, mybir.dt.from_np(v.dtype), kind="ExternalInput").ap()
           for k, v in arrays.items()}
    out = nc.dram_tensor("out_x", (SEQS, SEQ, DIM), F32, kind="ExternalOutput").ap()
    slots_in = nc.dram_tensor("slots_in", (SLOT_TILES * P, DIM), F32, kind="Internal").ap()
    slots_out = nc.dram_tensor("slots_out", (SLOT_TILES * P, DIM), F32, kind="Internal").ap()
    decoder(nc, ins, out, slots_in, slots_out)
    r = run_bass_kernel_spmd(nc, [{f"in_{k}": v for k, v in arrays.items()}], core_ids=[0])
    return r.results[0]["out_x"]
```

```python
import concourse.bass as bass
from concourse import mybir
from collections import namedtuple
from contextlib import ExitStack

F32 = mybir.dt.float32
BF16 = mybir.dt.bfloat16
F16 = mybir.dt.float16
I32 = mybir.dt.int32
ALU = mybir.AluOpType
ACT = mybir.ActivationFunctionType
AX = mybir.AxisListType

P = 128
SEQS, SEQ, DIM, HEADS, HD = 64, 64, 128, 16, 8
TOKENS = SEQS * SEQ
TILES = TOKENS // P
TPU = 2
UNITS = TILES // TPU
COLS = TPU * P
LAYERS = 3
EPS = 1e-5
SCALE = HD ** -0.5
HALF = HEADS // 2
PAIRS = HEADS // 2
EXPERTS, HID = 8, 512
POOL_HEADS = 5
CHUNKS = HID // P
W_SCALE, X_SCALE, H_SCALE = 64.0, 8.0, 16.0
SLOT_TILES = (TOKENS - EXPERTS) // P + EXPERTS
REGION = TOKENS + P
SLOT_ROWS = EXPERTS // 2 * REGION + (SLOT_TILES - TILES) * P
RING = 3
WEIGHTS = 9
GROUPS = 4
GT = TILES // GROUPS
RUN = 2 * RING
PEELED = 3 * RING
SPARE = RUN * P
assert SLOT_TILES % RING == 0 and (SLOT_TILES - PEELED) % RUN == 0

Unit = namedtuple("Unit", "layer u n least")

CONST = {}
CONST_COLS = 0
for _name, _n in (("ident", P), ("pick", P), ("head_mask", HALF), ("dist_qk", SEQ), ("cos", SEQ), ("sin", SEQ), ("before", P),
                  ("first", EXPERTS), ("slot128", TILES), ("tile_no", SLOT_TILES), ("slot_sign", EXPERTS),
                  ("slot_base", EXPERTS), ("tile_step", EXPERTS), ("tile_base", SLOT_TILES * EXPERTS),
                  ("idle_row", SLOT_TILES), ("token", TILES), ("spare", RUN)):
    CONST[_name] = (CONST_COLS, CONST_COLS + _n)
    CONST_COLS += _n


def decoder(nc, ins, out, slots, results):
    with ExitStack() as ctx:
        def sb(name, shape, dt=F32):
            return ctx.enter_context(nc.sbuf_tensor(name, shape, dt))

        def whole(name, shape, dt=F32):
            return sb(name, shape, dt)[tuple(slice(None) for _ in shape)]

        def sem(name):
            return ctx.enter_context(nc.semaphore(name))

        consts = sb("consts", [P, CONST_COLS])

        def const(name):
            a, b = CONST[name]
            return consts[:, a:b]

        ident = const("ident")
        x = sb("x", [P, TILES, DIM])
        y = sb("y", [P, TILES, DIM])
        z = sb("z", [P, TILES, DIM + 1])
        ctx_in = sb("ctx_in", [P, 2, TPU, DIM])
        wqkv = sb("wqkv", [P, LAYERS, 3, DIM])
        wrot = sb("wrot", [P, 2, DIM])
        wo = sb("wo", [P, LAYERS, DIM])
        cols = sb("cols", [P, 6])
        rows = sb("rows", [P, 2, DIM])
        bv = sb("bv", [P, DIM // 2])
        slopes = sb("slopes", [P, HEADS])
        gate_w = sb("gate_w", [P, EXPERTS])
        gate_b = sb("gate_b", [P, EXPERTS])
        w1 = sb("w1", [P, EXPERTS * HID])
        w2 = sb("w2", [P, EXPERTS * HID])
        pick16 = sb("pick16", [P, P], F16)
        alibi_qk = sb("alibi_qk", [P, HEADS, SEQ], F16)
        stats = sb("stats", [P, TPU, 6])
        mom = sb("mom", [P, TPU, 2])
        veps = sb("veps", [P, TPU])
        rstd = sb("rstd", [P, TPU])
        stats2 = sb("stats2", [P, TPU, 6])
        mom2 = sb("mom2", [P, TPU, 2])
        veps2 = sb("veps2", [P, TPU])
        rstd2 = sb("rstd2", [P, TPU])
        mhalf = sb("mhalf", [P, TPU])
        eps = sb("eps", [P, TPU])
        carrier = sb("carrier", [P, 1])
        xn = sb("xn", [P, TPU, DIM])
        xT = sb("xT", [P, COLS])
        cT = sb("cT", [P, COLS])
        rope_a = sb("rope_a", [P, 2 * COLS])
        rope_b = sb("rope_b", [P, 2 * COLS])
        qkT = sb("qkT", [P, 2, 2, COLS])
        km = sb("km", [P, 2, HALF, COLS])
        vb = sb("vb", [P, 2, TPU, 2, PAIRS, 2 * HD + 2])
        mrow = sb("mrow", [P, TPU, HEADS])
        prob = sb("prob", [P, TPU, HEADS * SEQ])
        probT = sb("probT", [P, TPU, PAIRS, P])
        oT = sb("oT", [P, 2 * COLS])
        rc = sb("rc", [P, TPU * PAIRS, 2])
        on = sb("on", [P, TPU, DIM])
        hT = sb("hT", [P, COLS])
        zT = whole("zT", [P, 2, GT // 2 * P])
        xs = whole("xs", [P, RING, DIM + 1])
        result_row = sb("result_row", [P, RUN], I32)
        pool_carrier = sb("pool_carrier", [P, 1])
        act_carrier = sb("act_carrier", [P, 1])
        xsT = whole("xsT", [P, RING, P])
        xs_hi = whole("xs_hi", [P, RING, P], F16)
        xs_lo = whole("xs_lo", [P, RING, P], F16)
        hs = whole("hs", [P, RING, HID])
        hs_hi = whole("hs_hi", [P, RING, HID], F16)
        hs_lo = whole("hs_lo", [P, RING, HID], F16)
        w1_parts = km[:, :, :, :].rearrange("p a h c -> p (a h c)").bitcast(F16)
        w1_hi, w1_lo = (w1_parts[:, k * EXPERTS * HID:(k + 1) * EXPERTS * HID] for k in range(2))
        w2_parts = whole("w2_parts", [P, EXPERTS * CHUNKS, 2, DIM], F16)
        w2_hi, w2_lo = (w2_parts[:, :, k, :] for k in range(2))
        w2_both = w2_parts.rearrange("p b k d -> p (b k d)")
        ln2_scaled = sb("ln2_scaled", [P, 2])
        ys = whole("ys", [P, RING, DIM])
        gstats = whole("gstats", [P, TILES, 6])
        gmom = whole("gmom", [P, TILES, 2])
        gveps = whole("gveps", [P, TILES])
        grstd = whole("grstd", [P, TILES])
        logits = whole("logits", [P, GT, EXPERTS])
        best = whole("best", [P, GT])
        tie = whole("tie", [P, GT, EXPERTS])
        tie_best = whole("tie_best", [P, GT])
        place = whole("place", [P, 2, GT, EXPERTS])
        slot_f = whole("slot_f", [P, GT])
        filled = whole("filled", [P, EXPERTS, TILES])
        used = whole("used", [P, EXPERTS])
        ends = whole("ends", [P, 2, EXPERTS])
        starts = whole("starts", [P, EXPERTS])
        passed = whole("passed", [P, SLOT_TILES, EXPERTS])
        begun = whole("begun", [P, SLOT_TILES, EXPERTS])
        nth = whole("nth", [P, SLOT_TILES, EXPERTS])
        expert_f = whole("expert_f", [P, SLOT_TILES])
        row_f = whole("row_f", [P, SLOT_TILES])
        zero = sb("zero", [P, DIM + 1])
        no_count = sb("no_count", [P, (TILES + 1) * EXPERTS], BF16)
        onehot = sb("onehot", [P, TILES, EXPERTS], BF16)
        before = sb("before", [P, P], BF16)
        ones = sb("ones", [P, P], BF16)
        slot = sb("slot", [P, TILES], I32)
        expert = sb("expert", [P, SLOT_TILES], I32)
        first_row = sb("first_row", [P, SLOT_TILES], I32)

        psum = ctx.enter_context(nc.psum_tensor("psum", [P, 8, 512], F32))
        s_ps = [psum[:, 2 * t:2 * t + 2, :].rearrange("p a c -> p (a c)") for t in range(TPU)]
        pv_ps = psum[:, 4, :]
        m0 = psum[:, 5, :]
        m1 = psum[:, 6, :]
        m2 = psum[:, 7, :]
        rank = m1[:, 0:(TILES + 1) * EXPERTS]

        c_in, w_in, moe_in = sem("c_in"), sem("w_in"), sem("moe_in")
        x_in, x_rest_in = sem("x_in"), sem("x_rest_in")
        ctx_sem = [sem("ctx_in0"), sem("ctx_in1")]
        ctx_used = sem("ctx_used")
        setup = sem("setup")
        setup_pool = sem("setup_pool")
        alibi_step = sem("alibi_step")
        d_stats, d_mom, d_xn = sem("d_stats"), sem("d_mom"), sem("d_xn")
        d_stats2, d_mom2, d_y = sem("d_stats2"), sem("d_mom2"), sem("d_y")
        d_max, d_sub = sem("d_max"), sem("d_sub")
        d_rope, d_qk, v_ready = sem("d_rope"), sem("d_qk"), sem("v_ready")
        d_rc, d_on, d_res = sem("d_rc"), sem("d_on"), sem("d_res")
        p_xT, p_qk, p_rot, p_v = sem("p_xT"), sem("p_qk"), sem("p_rot"), sem("p_v")
        p_s, p_pT, p_pv = sem("p_s"), sem("p_pT"), sem("p_pv")
        p_t1, p_t2, p_out = sem("p_t1"), sem("p_t2"), sem("p_out")
        a_xT, a_qk, a_exp, a_pT = sem("a_xT"), sem("a_qk"), sem("a_exp"), sem("a_pT")
        a_oT, a_hT, a_km = sem("a_oT"), sem("a_hT"), sem("a_km")
        g_veps, g_rstd, g_km, g_bias = sem("g_veps"), sem("g_rstd"), sem("g_km"), sem("g_bias")
        g_veps2, g_rstd2 = sem("g_veps2"), sem("g_rstd2")
        stored = sem("stored")
        zeroed = sem("zeroed")
        r_stats, r_mom, r_veps, r_rstd = sem("r_stats"), sem("r_mom"), sem("r_veps"), sem("r_rstd")
        r_z, r_zT, r_zT_sb = sem("r_z"), sem("r_zT"), sem("r_zT_sb")
        r_logits, route, counted, routed = sem("r_logits"), sem("route"), sem("counted"), sem("routed")
        table, tables, scattered, xy_sum = sem("table"), sem("tables"), sem("scattered"), sem("xy_sum")
        e_in = [sem(f"e_in{r}") for r in range(RING)]
        e_out = [sem(f"e_out{r}") for r in range(RING)]
        scaled, w_hi, w_lo = sem("scaled"), sem("w_hi"), sem("w_lo")
        e_xT, e_xT_sb, e_x, e_up = sem("e_xT"), sem("e_xT_sb"), sem("e_x"), sem("e_up")
        e_gelu, e_h_hi, e_h, e_down, e_y = sem("e_gelu"), sem("e_h_hi"), sem("e_h"), sem("e_down"), sem("e_y")
        returned = [sem(f"returned{g}") for g in range(GROUPS)]
        summed, carried = sem("summed"), sem("carried")


        def unit(layer, u, least=None):
            least = u if least is None else least
            if least < 0:
                layer, u, least = layer - 1, u + UNITS, least + UNITS
            return Unit(layer, u, layer * UNITS + u, layer * UNITS + least) if 0 <= layer < LAYERS else None

        def pipeline(eng, step, drained):
            for layer in range(LAYERS + 1):
                for u in range(4 if layer < LAYERS else 3):
                    step(*(unit(layer, u - k) for k in range(4)), u % 2)
                    if layer == LAYERS:
                        drained(u)
                if layer < LAYERS:
                    with eng.Fori(2, UNITS // 2) as i:
                        for par in (0, 1):
                            step(*(unit(layer, 2 * i + (par - k), 4 + par - k) for k in range(4)), par)

        def behind(s, least, lag, end):
            if least < lag or (isinstance(s, int) and s - lag >= end):
                return None
            return s - lag

        def expert_pipeline(eng, step, lag):
            for s in range(PEELED):
                step(s, s, s % RING, s // RING, s % RING, RING)
            with eng.Fori(0, (SLOT_TILES - PEELED) // RUN) as i:
                for k in range(PEELED, PEELED + RUN):
                    step(RUN * i + k, k, k % RING, (RUN // RING) * i + k // RING, k - PEELED, RUN)
            for s in range(SLOT_TILES, SLOT_TILES + lag):
                step(s, s, s % RING, s // RING, s - SLOT_TILES, RING)

        def tok(par_t, b):
            return slice(par_t * P + b * SEQ, par_t * P + (b + 1) * SEQ)

        block = ctx.enter_context(nc.Block())

        @block.sync
        def _(sp):
            sp.dma_start(consts[:, :], ins["consts"]).then_inc(c_in, 16)
            xv = ins["x"].rearrange("(t r) s d -> (r s) t d", r=2)
            sp.dma_start(x[:, 0:4, :], xv[:, 0:4, :]).then_inc(x_in, 16)
            for dst, name in ((wqkv[:, :, :, :].rearrange("p a b c -> p (a b c)"), "wqkv"),
                              (wrot[:, :, :].rearrange("p a c -> p (a c)"), "wrot"), (cols[:, :], "cols"),
                              (rows[:, :, :].rearrange("p a c -> p (a c)"), "rows"), (slopes[:, :], "slopes"),
                              (wo[:, :, :].rearrange("p a c -> p (a c)"), "wo"), (bv[:, :], "bv"),
                              (gate_w[:, :], "gate_w"), (gate_b[:, :], "gate_b")):
                sp.dma_start(dst, ins[name]).then_inc(w_in, 16)
            sp.dma_start(x[:, 4:TILES, :], xv[:, 4:TILES, :]).then_inc(x_rest_in, 16)
            sp.dma_start(w1[:, :], ins["w1"]).then_inc(moe_in, 16)
            sp.dma_start(w2[:, :], ins["w2"]).then_inc(moe_in, 16)
            cv = ins["ctx"].rearrange("(u t r) s d -> u (r s) t d", r=2, t=TPU)
            for u in (0, 1):
                sp.dma_start(ctx_in[:, u, :, :], cv[u]).then_inc(ctx_sem[u], 16)
            sp.wait_ge(setup_pool, 3)
            sp.dma_start(slots.rearrange("(t p) d -> p t d", p=P),
                         zero[:, None, :].broadcast_to([P, SLOT_ROWS // P, DIM + 1])).then_inc(zeroed, 16)
            sp.dma_start(results[0:SPARE, :].rearrange("(t p) d -> p t d", p=P),
                         zero[:, None, 0:DIM].broadcast_to([P, RUN, DIM])).then_inc(zeroed, 16)
            with sp.Fori(1, UNITS // 2) as i:
                for par in (0, 1):
                    sp.wait_ge(ctx_used, 2 * i + (par - 1))
                    sp.dma_start(ctx_in[:, par, :, :], cv[2 * i + par]).then_inc(ctx_sem[par], 16)

            sp.wait_ge(scattered, 16 * TILES)
            sp.wait_ge(tables, 1)

            def step(s, least, r, turn, at, run):
                j = behind(s, least, 0, SLOT_TILES)
                if j is not None:
                    if least >= RING:
                        sp.wait_ge(e_x, j - RING + 1)
                    row = sp.value_load(first_row[0:1, bass.ds(j, 1)], min_val=0, max_val=SLOT_ROWS - P)
                    sp.dma_start(xs[:, r, :], slots[bass.ds(row, P), :]).then_inc(e_in[r], 16)

            expert_pipeline(sp, step, 0)
            for r in range(RING):
                sp.wait_ge(e_out[r], 16 * SLOT_TILES // RING)
            sp.wait_ge(xy_sum, 1)
            rv = results[SPARE:SPARE + TOKENS, :].rearrange("(t p) d -> p t d", p=P)
            ov = out.rearrange("(t r) s d -> (r s) t d", r=2)
            for g in range(GROUPS):
                part = slice(g * GT, (g + 1) * GT)
                sp.dma_start(y[:, part, :], rv[:, part, :]).then_inc(returned[g], 16)
            for g in range(GROUPS):
                part = slice(g * GT, (g + 1) * GT)
                sp.wait_ge(summed, g + 1)
                sp.dma_start(ov[:, part, :], y[:, part, :]).then_inc(stored, 16)
            sp.wait_ge(stored, 16 * GROUPS)

        @block.gpsimd
        def _(pool):
            nc.gpsimd.memset(mhalf[:, :], -0.5).then_inc(setup_pool, 1)
            nc.gpsimd.memset(eps[:, :], EPS).then_inc(setup_pool, 1)
            nc.gpsimd.memset(zero[:, :], 0.0).then_inc(setup_pool, 1)
            pool.wait_ge(setup_pool, 3)
            pool.wait_ge(c_in, 16)

            def keys_apart(F, par, heads):
                for h in heads:
                    if h == 0:
                        last = nc.gpsimd.tensor_tensor(km[:, par, 0, :], qkT[:, par, 1, :],
                                                       const("head_mask")[:, 0:1].broadcast_to([P, COLS]), ALU.mult)
                    else:
                        last = nc.gpsimd.tensor_scalar(km[:, par, h, :], qkT[:, par, 1, :],
                                                       const("head_mask")[:, h:h + 1], 1.0, ALU.mult, ALU.mult)
                return last

            def step(G, F, C, B, par):
                if G is not None:
                    n = G.n
                    pool.wait_ge(d_mom, 2 * n + 2)
                    nc.gpsimd.tensor_tensor(veps[:, :], mom[:, :, 1], eps[:, :], ALU.add).then_inc(g_veps, 1)
                    pool.wait_ge(g_veps, n + 1)
                    nc.gpsimd.tensor_tensor(rstd[:, :], veps[:, :], mhalf[:, :], ALU.pow).then_inc(g_rstd, 1)
                if F is not None:
                    f = F.n
                    pool.wait_ge(a_qk if F.layer else d_qk, f + 1 - (UNITS if F.layer else 0))
                    if F.least > 1:
                        pool.wait_ge(p_s, 2 * f - 2)
                    keys_apart(F, 1 - par, range(3))
                if G is not None and G.layer == 2:
                    m = G.u
                    pool.wait_ge(d_mom2, 2 * m + 2)
                    nc.gpsimd.tensor_tensor(veps2[:, :], mom2[:, :, 1], eps[:, :], ALU.add).then_inc(g_veps2, 1)
                    pool.wait_ge(g_veps2, m + 1)
                    nc.gpsimd.tensor_tensor(rstd2[:, :], veps2[:, :], mhalf[:, :], ALU.pow).then_inc(g_rstd2, 1)
                if F is not None:
                    keys_apart(F, 1 - par, range(3, POOL_HEADS)).then_inc(g_km, 1)
                if G is not None and G.layer < 2:
                    if G.least == 0:
                        pool.wait_ge(w_in, 16 * WEIGHTS)
                    pool.wait_ge(d_xn, n + 1)
                    here = x[:, bass.ds(TPU * G.u, TPU), :]
                    nc.gpsimd.tensor_tensor(here, here, rows[:, G.layer, None, :].broadcast_to([P, TPU, DIM]),
                                            ALU.add).then_inc(g_bias, 1)

            def gate_rstd(g):
                tiles = slice(g * GT, (g + 1) * GT)
                pool.wait_ge(r_mom, g + 1)
                nc.gpsimd.tensor_tensor(gveps[:, tiles], gmom[:, tiles, 1], eps[:, 0:1].broadcast_to([P, GT]),
                                        ALU.add).then_inc(r_veps, 1)
                pool.wait_ge(r_veps, g + 1)
                nc.gpsimd.tensor_tensor(grstd[:, tiles], gveps[:, tiles], mhalf[:, 0:1].broadcast_to([P, GT]),
                                        ALU.pow).then_inc(r_rstd, 1)

            def scatter(g):
                pool.wait_ge(routed, g + 1)
                for t in range(g * GT, (g + 1) * GT):
                    nc.gpsimd.indirect_dma_start(out=slots, out_offset=bass.IndirectOffsetOnAxis(ap=slot[:, t:t + 1], axis=0),
                                                 in_=z[:, t, :], in_offset=None).then_inc(scattered, 16)

            pipeline(pool, step, lambda k: None)
            for g in range(GROUPS - 1):
                gate_rstd(g)
            pool.wait_ge(zeroed, 32)
            scatter(0)
            gate_rstd(GROUPS - 1)
            for g in range(1, GROUPS):
                scatter(g)

            def expert_step(s, least, r, turn, at, run):
                j = behind(s, least, 0, SLOT_TILES)
                if j is not None:
                    pool.wait_ge(e_y, j + 1)
                    if least:
                        pool.wait_ge(carried, j)
                    nc.gpsimd.tensor_tensor(pool_carrier[:, :], eps[:, 0:1], eps[:, 1:2], ALU.add).then_inc(carried, 1)
                    k = least % RUN
                    nc.gpsimd.indirect_dma_start(
                        out=results, out_offset=bass.IndirectOffsetOnAxis(ap=result_row[:, k:k + 1], axis=0),
                        in_=ys[:, r, :], in_offset=None).then_inc(e_out[r], 16)

            expert_pipeline(pool, expert_step, 0)

        @block.scalar
        def _(act):
            def transposed(U, t):
                n = U.n
                act.wait_ge(p_pT, 2 * n + t + 1)
                nc.scalar.activation(probT[:, t, :, :].rearrange("p a q -> p (a q)"), s_ps[t], ACT.Copy).then_inc(a_pT, 1)

            def exponentials(U, t):
                n = U.n
                act.wait_ge(d_sub, 2 * n + t + 1)
                nc.scalar.activation(prob[:, t, :], prob[:, t, :], ACT.Exp, scale=SCALE).then_inc(a_exp, 1)

            def keys_apart(F, par, heads):
                for h in heads:
                    last = nc.scalar.activation(km[:, par, h, :], qkT[:, par, 1, :], ACT.Copy,
                                                scale=const("head_mask")[:, h:h + 1])
                return last

            def step(G, F, C, B, par):
                fpar = 1 - par
                if F is not None:
                    f = F.n
                    if F.layer:
                        act.wait_ge(p_qk, f + 1)
                        act.wait_ge(p_s, 2 * f - 2)
                        act.wait_ge(g_km, f - 1)
                        if F.layer == 1:
                            for i in range(2):
                                last = nc.scalar.activation(qkT[:, fpar, i, :], m1[:, i * COLS:(i + 1) * COLS],
                                                            ACT.Identity, bias=cols[:, i:i + 1])
                        else:
                            last = nc.scalar.activation(qkT[:, fpar, :, :].rearrange("p a c -> p (a c)"), m1, ACT.Copy)
                        last.then_inc(a_qk, 1)
                if B is not None:
                    transposed(B, 1)
                if F is not None:
                    act.wait_ge(a_qk if F.layer else d_qk, f + 1 - (UNITS if F.layer else 0))
                    if F.least > 1:
                        act.wait_ge(p_s, 2 * f - 2)
                    keys_apart(F, fpar, range(POOL_HEADS, HALF - 1))
                if B is not None:
                    b_ = B.n
                    act.wait_ge(p_pv, 2 * b_ + 2)
                    if B.least:
                        act.wait_ge(p_t1, b_)
                    nc.scalar.activation(oT[:, :], pv_ps, ACT.Copy).then_inc(a_oT, 1)
                if F is not None:
                    keys_apart(F, fpar, range(HALF - 1, HALF)).then_inc(a_km, 1)
                if C is not None:
                    exponentials(C, 0)
                if F is not None and F.layer != 1:
                    act.wait_ge(p_v, f + 1)
                    if F.least > 1:
                        act.wait_ge(p_pv, 2 * f - 2)
                    for odd in range(2):
                        part = slice(64 * odd, 64 * odd + 64)
                        src = m0[part, 0:COLS].rearrange("p (a k d) -> p a k d", k=PAIRS, d=HD)
                        dst = vb[part, fpar, :, :, :, HD * odd:HD * odd + HD].rearrange("p t b k d -> p (t b) k d")
                        last = nc.scalar.activation(dst, src, ACT.Copy)
                    last.then_inc(v_ready, 1)
                if B is not None:
                    act.wait_ge(p_t2, b_ + 1)
                    if B.least:
                        act.wait_ge(p_out, b_)
                    nc.scalar.activation(hT[:, :], m2[:, 0:COLS], ACT.Copy).then_inc(a_hT, 1)
                if G is not None:
                    n = G.n
                    act.wait_ge(p_xT, n + 1)
                    if G.least:
                        act.wait_ge(p_v, n)
                    if G.layer == 1:
                        nc.scalar.activation(cT[:, :], m1[:, COLS:2 * COLS], ACT.Copy)
                    if G.layer == 2:
                        nc.scalar.activation(xT[:, :], m1[:, 0:COLS], ACT.Identity, bias=cols[:, 3:4],
                                             scale=cols[:, 2:3]).then_inc(a_xT, 1)
                    else:
                        nc.scalar.activation(xT[:, :], m1[:, 0:COLS], ACT.Copy).then_inc(a_xT, 1)
                if C is not None:
                    transposed(C, 0)
                    exponentials(C, 1)

            act.wait_ge(c_in, 16)
            act.wait_ge(setup, 1)
            act.wait_ge(w_in, 16 * WEIGHTS)
            def gate_zT(g):
                for half in range(2):
                    act.wait_ge(r_zT, 2 * g + half + 1)
                    nc.scalar.activation(zT[:, half, :], s_ps[0][:, half * 512:(half + 1) * 512], ACT.Identity, bias=cols[:, 5:6],
                                         scale=cols[:, 4:5]).then_inc(r_zT_sb, 1)

            def large_part(w, hi):
                nc.scalar.activation(hi, w, ACT.Copy, scale=W_SCALE).then_inc(w_hi, 1)

            def drained(k):
                for g in ((), (0,), (1, 2, 3))[k]:
                    gate_zT(g)
                if k == 0:
                    act.wait_ge(moe_in, 32)
                    large_part(w2[:, :].rearrange("p (b d) -> p b d", d=DIM), w2_hi)
                elif k == 1:
                    act.wait_ge(p_s, 2 * LAYERS * UNITS)
                    large_part(w1[:, :], w1_hi)

            pipeline(act, step, drained)
            act.wait_ge(setup_pool, 3)
            nc.scalar.activation(act_carrier[:, :], eps[:, 0:1], ACT.Gelu_apprx_tanh)

            def expert_step(s, least, r, turn, at, run):
                j = behind(s, least, 0, SLOT_TILES)
                if j is not None:
                    act.wait_ge(e_xT, j + 1)
                    for dst in (xsT, xs_hi):
                        last = nc.scalar.activation(dst[:, r, :], psum[:, 6, 0:P], ACT.Identity, bias=ln2_scaled[:, 1:2],
                                                    scale=ln2_scaled[:, 0:1])
                    last.then_inc(e_xT_sb, 1)
                j = behind(s, least, 1, SLOT_TILES)
                if j is not None:
                    q = (r - 1) % RING
                    act.wait_ge(e_up, j + 1)
                    nc.scalar.activation(hs[:, q, :], psum[:, q, :], ACT.Gelu_apprx_tanh,
                                         scale=1.0 / (W_SCALE * X_SCALE)).then_inc(e_gelu, 1)

            act.wait_ge(scaled, 1)
            expert_pipeline(act, expert_step, 1)

        @block.vector
        def _(dve):
            nc.vector.memset(vb[:, :, :, :, :, :], 0.0).then_inc(alibi_step, 1)
            nc.vector.memset(pv_ps, 0.0)
            dve.wait_ge(alibi_step, 1)
            nc.vector.memset(vb[0:64, :, :, :, :, 16:17], 1.0)
            nc.vector.memset(vb[64:128, :, :, :, :, 17:18], 1.0).then_inc(setup, 1)
            dve.wait_ge(c_in, 16)
            nc.vector.tensor_copy(pick16[:, :], const("pick")).then_inc(setup, 1)
            def late_setup():
                dve.wait_ge(w_in, 16 * WEIGHTS)
                exact = prob[:, 0, :].rearrange("p (h s) -> p h s", h=HEADS)
                nc.vector.tensor_tensor(exact, const("dist_qk")[:, None, :].broadcast_to([P, HEADS, SEQ]),
                                        slopes[:, :, None].broadcast_to([P, HEADS, SEQ]), ALU.mult).then_inc(alibi_step, 1)
                dve.wait_ge(alibi_step, 2)
                nc.vector.tensor_copy(alibi_qk[:, :, :], exact).then_inc(alibi_step, 1)
                dve.wait_ge(alibi_step, 3)
                nc.vector.tensor_tensor(alibi_qk[64:128, :, :], exact[64:128, :, :], alibi_qk[64:128, :, :],
                                        ALU.subtract).then_inc(alibi_step, 1)
                dve.wait_ge(alibi_step, 4)
                nc.vector.tensor_scalar(ln2_scaled[:, :], cols[:, 4:6], X_SCALE, None, ALU.mult).then_inc(scaled, 1)
                nc.vector.tensor_copy(z[:, :, :].bitcast(I32)[:, :, DIM], const("token"))
                nc.vector.tensor_copy(before[:, :], const("before"))
                nc.vector.memset(ones[:, :], 1.0)
                nc.vector.memset(no_count[:, :], 0.0).then_inc(setup, 1)

            def maxima(C, t):
                dve.wait_ge(p_s, 2 * C.n + t + 1)
                nc.vector.tensor_reduce(mrow[:, t, :], s_ps[t].rearrange("p (h s) -> p h s", h=HEADS), AX.X,
                                        ALU.max).then_inc(d_max, 1)

            def subtract(C, t):
                dve.wait_ge(d_max, 2 * C.n + t + 1)
                nc.vector.tensor_tensor(prob[:, t, :].rearrange("p (h s) -> p h s", h=HEADS),
                                        s_ps[t].rearrange("p (h s) -> p h s", h=HEADS),
                                        mrow[:, t, :, None].broadcast_to([P, HEADS, SEQ]), ALU.subtract).then_inc(d_sub, 1)

            def step(G, F, C, B, par):
                fpar = 1 - par
                if G is not None:
                    n = G.n
                    if G.layer == 0:
                        dve.wait_ge(x_in if G.least < 2 else x_rest_in, 16)
                    else:
                        dve.wait_ge(d_res, n - UNITS + 1)
                    if G.least:
                        dve.wait_ge(g_veps, n)
                        dve.wait_ge(p_xT, n)
                        nc.vector.memset(carrier[:, :], 0.0)
                    for t in range(TPU):
                        nc.vector.bn_stats(stats[:, t, :], x[:, TPU * G.u + t, :]).then_inc(d_stats, 1)
                    dve.wait_ge(d_stats, 2 * n + 2)
                    nc.vector.memset(carrier[:, :], 0.0)
                    for t in range(TPU):
                        nc.vector.bn_aggr(mom[:, t, :], stats[:, t, :]).then_inc(d_mom, 1)
                if F is not None and F.layer == 0:
                    f = F.n
                    dve.wait_ge(p_qk, f + 1)
                    tab = lambda name: const(name)[:, None, :].broadcast_to([P, 2 * COLS // SEQ, SEQ])
                    blocks = lambda ap: ap.rearrange("p (b s) -> p b s", s=SEQ)
                    if F.least:
                        dve.wait_ge(d_qk, f)
                    nc.vector.tensor_tensor(blocks(rope_a[:, :]), blocks(m1), tab("cos"), ALU.mult).then_inc(d_rope, 1)
                    dve.wait_ge(p_rot, f + 1)
                    nc.vector.tensor_tensor(blocks(rope_b[:, :]), blocks(m0), tab("sin"), ALU.mult).then_inc(d_rope, 1)
                    dve.wait_ge(d_rope, 2 * f + 2)
                    if F.least > 1:
                        dve.wait_ge(p_s, 2 * f - 2)
                        dve.wait_ge(g_km, f - 1)
                        dve.wait_ge(a_km, f - 1)
                    nc.vector.tensor_tensor(qkT[:, fpar, :, :].rearrange("p a c -> p (a c)"), rope_a[:, :], rope_b[:, :],
                                            ALU.add).then_inc(d_qk, 1)
                if G is not None:
                    dve.wait_ge(g_rstd, n + 1)
                    dst = (lambda t: y[:, TPU * G.u + t, :]) if G.layer == 2 else (lambda t: xn[:, t, :])
                    for t in range(TPU):
                        last = nc.vector.tensor_scalar(dst(t), x[:, TPU * G.u + t, :], mom[:, t, 0:1], rstd[:, t:t + 1],
                                                       ALU.subtract, ALU.mult)
                    if G.layer != 2:
                        last.then_inc(d_xn, 1)
                    else:
                        m = G.u
                        last.then_inc(d_y, 1)
                        dve.wait_ge(d_y, m + 1)
                        nc.vector.memset(carrier[:, :], 0.0)
                        for t in range(TPU):
                            nc.vector.bn_stats(stats2[:, t, :], y[:, TPU * G.u + t, :]).then_inc(d_stats2, 1)
                        dve.wait_ge(d_stats2, 2 * m + 2)
                        nc.vector.memset(carrier[:, :], 0.0)
                        for t in range(TPU):
                            nc.vector.bn_aggr(mom2[:, t, :], stats2[:, t, :]).then_inc(d_mom2, 1)
                if C is not None:
                    maxima(C, 0)
                    subtract(C, 0)
                if G is not None and G.layer == 2:
                    dve.wait_ge(g_rstd2, m + 1)
                    for t in range(TPU):
                        last = nc.vector.tensor_scalar(xn[:, t, :], y[:, TPU * G.u + t, :], mom2[:, t, 0:1],
                                                       rstd2[:, t:t + 1], ALU.subtract, ALU.mult)
                    last.then_inc(d_xn, 1)
                if B is not None:
                    b_ = B.n
                    dve.wait_ge(p_t1, b_ + 1)
                    t1 = m2.rearrange("p (g w) -> p g w", w=32)
                    nc.vector.reciprocal(rc[:, :, :], t1[:, :, 2 * HD:2 * HD + 2]).then_inc(d_rc, 1)
                    dve.wait_ge(d_rc, b_ + 1)
                    if B.least:
                        dve.wait_ge(p_t2, b_)
                    nc.vector.tensor_tensor(on[:, :, :].rearrange("p t (k o d) -> p (t k) o d", o=2, d=HD),
                                            t1[:, :, 0:2 * HD].rearrange("p g (o d) -> p g o d", o=2),
                                            rc[:, :, :, None].broadcast_to([P, TPU * PAIRS, 2, HD]), ALU.mult).then_inc(d_on, 1)
                if F is not None and F.layer == 1:
                    f = F.n
                    dve.wait_ge(p_v, f + 1)
                    if F.least > 1:
                        dve.wait_ge(p_pv, 2 * f - 2)
                    for odd in range(2):
                        part = slice(64 * odd, 64 * odd + 64)
                        src = m0[part, 0:COLS].rearrange("p (a k d) -> p a k d", k=PAIRS, d=HD)
                        dst = vb[part, fpar, :, :, :, HD * odd:HD * odd + HD].rearrange("p t b k d -> p (t b) k d")
                        bias = bv[part, :].rearrange("p (k d) -> p k d", d=HD)[:, None, :, :]
                        last = nc.vector.tensor_tensor(dst, src, bias.broadcast_to([64, 2 * TPU, PAIRS, HD]), ALU.add)
                    last.then_inc(v_ready, 1)
                if C is not None:
                    maxima(C, 1)
                    subtract(C, 1)
                if B is not None:
                    dve.wait_ge(p_out, b_ + 1)
                    if B.layer < 2:
                        dve.wait_ge(g_bias, b_ + 1)
                    here = (x if B.layer < 2 else y)[:, bass.ds(TPU * B.u, TPU), :]
                    nc.vector.tensor_tensor(here, here, m2[:, COLS:2 * COLS].rearrange("p (t d) -> p t d", t=TPU),
                                            ALU.add).then_inc(d_res, 1)
                if F is None and G is not None:
                    late_setup()

            def gate_moments(g):
                dve.wait_ge(d_res, 2 * UNITS + (g + 1) * GT // TPU)
                for t in range(g * GT, (g + 1) * GT):
                    nc.vector.bn_stats(gstats[:, t, :], y[:, t, :]).then_inc(r_stats, 1)
                dve.wait_ge(r_stats, (g + 1) * GT)
                for t in range(g * GT, (g + 1) * GT):
                    last = nc.vector.bn_aggr(gmom[:, t, :], gstats[:, t, :])
                last.then_inc(r_mom, 1)

            def gate_norm(g):
                dve.wait_ge(r_rstd, g + 1)
                for t in range(g * GT, (g + 1) * GT):
                    last = nc.vector.tensor_scalar(z[:, t, 0:DIM], y[:, t, :], gmom[:, t, 0:1], grstd[:, t:t + 1],
                                                   ALU.subtract, ALU.mult)
                last.then_inc(r_z, 1)

            GTE = [P, GT, EXPERTS]
            by_tile = lambda a: a[:, :, None].broadcast_to(GTE)
            by_expert = lambda a: a[:, None, :].broadcast_to(GTE)

            def choose(g):
                dve.wait_ge(r_logits, g + 1)
                nc.vector.tensor_tensor(logits, (m0, m2)[g % 2][:, 0:GT * EXPERTS].rearrange("p (t e) -> p t e", t=GT),
                                        by_expert(gate_b[:, :]), ALU.add).then_inc(route, 1)
                dve.wait_ge(route, 10 * g + 1)
                nc.vector.tensor_reduce(best, logits, AX.X, ALU.max).then_inc(route, 1)
                dve.wait_ge(route, 10 * g + 2)
                nc.vector.tensor_tensor(tie, logits, by_tile(best), ALU.is_ge).then_inc(route, 1)
                dve.wait_ge(route, 10 * g + 3)
                nc.vector.tensor_tensor(tie, tie, by_expert(const("first")), ALU.mult).then_inc(route, 1)
                dve.wait_ge(route, 10 * g + 4)
                nc.vector.tensor_reduce(tie_best, tie, AX.X, ALU.max).then_inc(route, 1)
                dve.wait_ge(route, 10 * g + 5)
                nc.vector.tensor_tensor(onehot[:, g * GT:(g + 1) * GT, :], tie, by_tile(tie_best),
                                        ALU.is_equal).then_inc(route, 1)

            def find_slots(g):
                tiles = slice(g * GT, (g + 1) * GT)
                dve.wait_ge(counted, g + 1)
                nc.vector.tensor_tensor(place[:, 0, :, :],
                                        rank[:, g * GT * EXPERTS:(g + 1) * GT * EXPERTS].rearrange("p (t e) -> p t e", t=GT),
                                        by_expert(const("slot_sign")), ALU.mult).then_inc(route, 1)
                dve.wait_ge(route, 10 * g + 7)
                nc.vector.tensor_tensor(place[:, 1, :, :], place[:, 0, :, :], by_expert(const("slot_base")),
                                        ALU.add).then_inc(route, 1)
                dve.wait_ge(route, 10 * g + 8)
                nc.vector.tensor_tensor(place[:, 0, :, :], place[:, 1, :, :], onehot[:, tiles, :], ALU.mult).then_inc(route, 1)
                dve.wait_ge(route, 10 * g + 9)
                nc.vector.tensor_reduce(slot_f, place[:, 0, :, :], AX.X, ALU.add).then_inc(route, 1)
                dve.wait_ge(route, 10 * g + 10)
                nc.vector.tensor_scalar(slot[:, tiles], slot_f, float(SLOT_ROWS - 1), 0.0, ALU.min, ALU.max).then_inc(routed, 1)

            def small_part(w, hi, lo, k):
                dve.wait_ge(w_hi, k)
                nc.vector.scalar_tensor_tensor(out=lo, in0=w, scalar=W_SCALE, in1=hi, op0=ALU.mult,
                                               op1=ALU.subtract).then_inc(w_lo, 1)

            def drained(k):
                if k == 0:
                    gate_moments(0)
                    gate_norm(0)
                elif k == 1:
                    gate_moments(1)
                    gate_norm(1)
                    choose(0)
                    find_slots(0)
                    gate_moments(2)
                else:
                    gate_moments(3)
                    gate_norm(2)
                    gate_norm(3)
                    choose(1)
                    find_slots(1)
                    small_part(w2[:, :].rearrange("p (b d) -> p b d", d=DIM), w2_hi, w2_lo, 1)
                    choose(2)
                    find_slots(2)
                    small_part(w1[:, :], w1_hi, w1_lo, 2)
                    choose(3)
                    find_slots(3)

            pipeline(dve, step, drained)

            STE = [P, SLOT_TILES, EXPERTS]
            of_tile = lambda a: a[:, :, None].broadcast_to(STE)
            of_expert = lambda a: a[:, None, :].broadcast_to(STE)
            nc.vector.tensor_tensor(filled, rank[:, TILES * EXPERTS:, None].broadcast_to([P, EXPERTS, TILES]),
                                    const("slot128")[:, None, :].broadcast_to([P, EXPERTS, TILES]),
                                    ALU.is_gt).then_inc(table, 1)
            dve.wait_ge(table, 1)
            nc.vector.tensor_reduce(used, filled, AX.X, ALU.add).then_inc(table, 1)
            dve.wait_ge(table, 2)
            nc.vector.tensor_copy(ends[:, 0, :], used).then_inc(table, 1)
            done, now, shift = 3, 0, 1
            while shift < EXPERTS:
                dve.wait_ge(table, done)
                nc.vector.tensor_copy(ends[:, 1 - now, 0:shift], ends[:, now, 0:shift])
                nc.vector.tensor_tensor(ends[:, 1 - now, shift:EXPERTS], ends[:, now, shift:EXPERTS],
                                        ends[:, now, 0:EXPERTS - shift], ALU.add).then_inc(table, 1)
                done, now, shift = done + 1, 1 - now, 2 * shift
            end = ends[:, now, :]
            dve.wait_ge(table, done)
            nc.vector.tensor_tensor(starts, end, used, ALU.subtract).then_inc(table, 1)
            nc.vector.tensor_tensor(passed, of_tile(const("tile_no")), of_expert(end), ALU.is_ge).then_inc(table, 1)
            dve.wait_ge(table, done + 2)
            nc.vector.tensor_tensor(begun, of_tile(const("tile_no")), of_expert(starts), ALU.is_ge).then_inc(table, 1)
            nc.vector.tensor_tensor(nth, of_tile(const("tile_no")), of_expert(starts), ALU.subtract).then_inc(table, 1)
            nc.vector.tensor_reduce(expert_f, passed, AX.X, ALU.add).then_inc(table, 1)
            dve.wait_ge(table, done + 5)
            nc.vector.tensor_tensor(begun, begun, passed, ALU.subtract).then_inc(table, 1)
            nc.vector.tensor_tensor(nth, nth, of_expert(const("tile_step")), ALU.mult).then_inc(table, 1)
            nc.vector.tensor_scalar(expert[:, :], expert_f, float(EXPERTS - 1), float(HID), ALU.min, ALU.mult)
            dve.wait_ge(table, done + 7)
            nc.vector.tensor_tensor(nth, nth, const("tile_base").rearrange("p (j e) -> p j e", e=EXPERTS),
                                    ALU.add).then_inc(table, 1)
            dve.wait_ge(table, done + 8)
            nc.vector.tensor_tensor(nth, nth, begun, ALU.mult).then_inc(table, 1)
            dve.wait_ge(table, done + 9)
            nc.vector.tensor_reduce(row_f, nth, AX.X, ALU.add).then_inc(table, 1)
            dve.wait_ge(table, done + 10)
            nc.vector.tensor_tensor(first_row[:, :], row_f, const("idle_row"), ALU.add).then_inc(tables, 1)

            nc.vector.tensor_tensor(x[:, :, :], x[:, :, :], y[:, :, :], ALU.add).then_inc(xy_sum, 1)

            def expert_step(s, least, r, turn, at, run):
                j = behind(s, least, 0, SLOT_TILES)
                if j is not None:
                    dve.wait_ge(e_xT_sb, j + 1)
                    if least >= RUN:
                        dve.wait_ge(e_out[r], 16 * (turn + 1 - RUN // RING))
                    k = least % RUN
                    nc.vector.tensor_tensor(result_row[:, k:k + 1], xs.bitcast(I32)[:, r, DIM:DIM + 1],
                                            const("spare")[:, k:k + 1], ALU.max)
                    nc.vector.tensor_tensor(xs_lo[:, r, :], xsT[:, r, :], xs_hi[:, r, :], ALU.subtract).then_inc(e_x, 1)
                j = behind(s, least, 1, SLOT_TILES)
                if j is not None:
                    q = (r - 1) % RING
                    dve.wait_ge(e_gelu, j + 1)
                    nc.vector.tensor_scalar(hs_hi[:, q, :], hs[:, q, :], H_SCALE, None, ALU.mult).then_inc(e_h_hi, 1)
                    dve.wait_ge(e_h_hi, j + 1)
                    nc.vector.scalar_tensor_tensor(out=hs_lo[:, q, :], in0=hs[:, q, :], scalar=H_SCALE, in1=hs_hi[:, q, :],
                                                   op0=ALU.mult, op1=ALU.subtract).then_inc(e_h, 1)
                j = behind(s, least, 2, SLOT_TILES)
                if j is not None:
                    q = (r - 2) % RING
                    dve.wait_ge(e_down, j + 1)
                    if least - 2 >= RING:
                        dve.wait_ge(e_out[q], 16 * (turn + (r - 2) // RING))
                    nc.vector.tensor_reduce(ys[:, q, :], psum[:, 3 + q, 0:2 * DIM].rearrange("p (k d) -> p d k", k=2),
                                            AX.X, ALU.add).then_inc(e_y, 1)

            expert_pipeline(dve, expert_step, 2)
            dve.wait_ge(xy_sum, 1)
            for g in range(GROUPS):
                part = slice(g * GT, (g + 1) * GT)
                dve.wait_ge(returned[g], 16)
                nc.vector.scalar_tensor_tensor(out=y[:, part, :], in0=y[:, part, :], scalar=1.0 / (W_SCALE * H_SCALE),
                                               in1=x[:, part, :], op0=ALU.mult, op1=ALU.add).then_inc(summed, 1)

        @block.tensor
        def _(pe):
            mm = nc.tensor.matmul

            def scores(C, t, par):
                n = C.n
                if t == 0:
                    pe.wait_ge(g_km, n + 1)
                    pe.wait_ge(a_km, n + 1)
                if C.least:
                    pe.wait_ge(a_pT, 2 * n + (t - 1))
                if C.layer:
                    mm(s_ps[t][0:64, 0:2], pick16[:, 0:64], pick16[:, 0:2], start=True, stop=True, skip_group_check=True)
                if C.layer == 0:
                    if C.least == 0:
                        pe.wait_ge(alibi_step, 4)
                    for half in range(2):
                        mm(s_ps[t][:, half * 512:(half + 1) * 512], pick16[:, :],
                           alibi_qk[:, half * HALF:(half + 1) * HALF, :], start=True, stop=False, skip_group_check=True)
                for half in range(2):
                    for b in range(2):
                        of_half = slice(64 * half, 64 * half + 64)
                        last = mm(s_ps[t][64 * b:64 * b + 64, half * 512:(half + 1) * 512], qkT[of_half, par, 0, tok(t, b)],
                                  km[of_half, par, :, tok(t, b)], start=C.layer != 0, stop=True,
                                  skip_group_check=True)
                last.then_inc(p_s, 1)

            def transposes(U, t):
                pe.wait_ge(a_exp, 2 * U.n + t + 1)
                for k in range(PAIRS):
                    last = mm(s_ps[t][:, k * P:(k + 1) * P], prob[:, t, k * P:(k + 1) * P], ident, is_transpose=True,
                              start=True, stop=True)
                last.then_inc(p_pT, 1)

            def values(U, t, par):
                n = U.n
                pe.wait_ge(a_pT, 2 * n + t + 1)
                if t == 0:
                    pe.wait_ge(v_ready, n + 1)
                    if U.least:
                        pe.wait_ge(a_oT, n)
                for k in range(PAIRS):
                    for b in range(2):
                        c, g = k % 4, 4 * t + 2 * (k // 4) + b
                        last = mm(pv_ps[32 * c:32 * c + 2 * HD + 2, g * SEQ:(g + 1) * SEQ], vb[:, par, t, b, k, :],
                                  probT[:, t, k, b * SEQ:(b + 1) * SEQ], start=True, stop=True, tile_position=(0, 32 * c))
                last.then_inc(p_pv, 1)

            def step(G, F, C, B, par):
                fpar = 1 - par
                if F is not None:
                    f = F.n
                    pe.wait_ge(a_xT, f + 1)
                    for i in range(2):
                        last = mm(m1[:, i * COLS:(i + 1) * COLS], wqkv[:, F.layer, i, :],
                                  cT[:, :] if i and F.layer == 1 else xT[:, :], start=True, stop=True)
                    last.then_inc(p_qk, 1)
                    if F.least:
                        pe.wait_ge(v_ready, f)
                    if F.layer == 0:
                        for i in range(2):
                            last = mm(m0[:, i * COLS:(i + 1) * COLS], wrot[:, i, :], xT[:, :], start=True, stop=True)
                        last.then_inc(p_rot, 1)
                if B is not None:
                    values(B, 0, fpar)
                    transposes(B, 1)
                if C is not None:
                    scores(C, 0, par)
                if B is not None:
                    values(B, 1, fpar)
                if F is not None:
                    if F.layer == 0:
                        pe.wait_ge(d_rope, 2 * f + 2)
                    for t in range(TPU):
                        for b in range(2):
                            for odd in range(2):
                                last = mm(m0[64 * odd:64 * odd + 64, (2 * t + b) * 64:(2 * t + b + 1) * 64],
                                          (cT if F.layer == 1 else xT)[:, tok(t, b)],
                                          wqkv[:, F.layer, 2, odd * 64:(odd + 1) * 64], start=True, stop=True)
                    last.then_inc(p_v, 1)
                if B is not None:
                    b_ = B.n
                    pe.wait_ge(a_oT, b_ + 1)
                    if B.least:
                        pe.wait_ge(d_res, b_)
                    for k in range(2 * TPU):
                        last = mm(m2[:, k * P:(k + 1) * P], oT[:, k * P:(k + 1) * P], ident, is_transpose=True,
                                  start=True, stop=True)
                    last.then_inc(p_t1, 1)
                if C is not None:
                    scores(C, 1, par)
                if B is not None:
                    pe.wait_ge(d_on, b_ + 1)
                    for t in range(TPU):
                        last = mm(m2[:, t * P:(t + 1) * P], on[:, t, :], ident, is_transpose=True, start=True, stop=True)
                    last.then_inc(p_t2, 1)
                if G is not None:
                    n = G.n
                    pe.wait_ge(d_xn, n + 1)
                    if F is not None:
                        if F.layer == 0:
                            pe.wait_ge(d_rope, 2 * f + 2)
                        else:
                            pe.wait_ge(a_qk, f - UNITS + 1)
                    if G.layer == 1:
                        pe.wait_ge(ctx_sem[par], 8 * (G.u - par) + 16)
                        for t in range(TPU):
                            last = mm(m1[:, COLS + t * P:COLS + (t + 1) * P], ctx_in[:, par, t, :], ident,
                                      is_transpose=True, start=True, stop=True)
                        last.then_inc(ctx_used, 1)
                    for t in range(TPU):
                        last = mm(m1[:, t * P:(t + 1) * P], xn[:, t, :], ident, is_transpose=True, start=True, stop=True)
                    last.then_inc(p_xT, 1)
                if C is not None:
                    transposes(C, 0)
                if B is not None:
                    pe.wait_ge(a_hT, b_ + 1)
                    for t in range(TPU):
                        last = mm(m2[:, COLS + t * P:COLS + (t + 1) * P], hT[:, t * P:(t + 1) * P], wo[:, B.layer, :],
                                  start=True, stop=True)
                    last.then_inc(p_out, 1)

            pe.wait_ge(c_in, 16)
            pe.wait_ge(w_in, 16 * WEIGHTS)
            pe.wait_ge(setup, 2)
            def gate_logits(g):
                pe.wait_ge(r_z, g + 1)
                for half in range(2):
                    if g:
                        pe.wait_ge(r_zT_sb, 2 * g - 1 + half)
                    elif half == 0:
                        pe.wait_ge(a_pT, 2 * LAYERS * UNITS - 1)
                    for t in range(GT // 2):
                        last = mm(s_ps[0][:, (half * GT // 2 + t) * P:(half * GT // 2 + t + 1) * P], z[:, g * GT + half * GT // 2 + t, 0:DIM], ident,
                                  is_transpose=True, start=True, stop=True)
                    last.then_inc(r_zT, 1)
                if g == 0:
                    pe.wait_ge(v_ready, LAYERS * UNITS)
                elif g == 1:
                    pe.wait_ge(d_res, LAYERS * UNITS)
                else:
                    pe.wait_ge(route, 10 * (g - 2) + 1)
                pe.wait_ge(r_zT_sb, 2 * g + 2)
                for t in range(GT):
                    k = t % (GT // 2)
                    last = mm((m0, m2)[g % 2][:, t * EXPERTS:(t + 1) * EXPERTS], zT[:, t // (GT // 2), k * P:(k + 1) * P], gate_w[:, :],
                              start=True, stop=True)
                last.then_inc(r_logits, 1)

            def count(g):
                pe.wait_ge(route, 10 * g + 6)
                if g == 0:
                    pe.wait_ge(a_qk, (LAYERS - 1) * UNITS)
                    pe.wait_ge(setup, 3)
                    mm(rank, ones[:, :], no_count[:, :], start=True, stop=False, skip_group_check=True)
                for t in range(g * GT, (g + 1) * GT):
                    mm(rank[:, t * EXPERTS:(t + 1) * EXPERTS], before[:, :], onehot[:, t, :], start=False, stop=False,
                       skip_group_check=True)
                    last = mm(rank[:, (t + 1) * EXPERTS:], ones[:, :],
                              onehot[:, t, None, :].broadcast_to([P, TILES - t, EXPERTS]), start=False, stop=True,
                              skip_group_check=True)
                last.then_inc(counted, 1)

            def drained(k):
                for part, g in ((), ((gate_logits, 0), (count, 0)),
                                ((gate_logits, 1), (gate_logits, 2), (count, 1), (gate_logits, 3), (count, 2), (count, 3)))[k]:
                    part(g)

            pipeline(pe, step, drained)

            def weight_columns(first, n):
                return nc.values_load_multi_w_load_instructions(expert[0:1, bass.ds(first, n)], engines=[mybir.EngineType.PE],
                                                                min_val=0, max_val=(EXPERTS - 1) * HID)[1]

            columns = {}

            def expert_step(s, least, r, turn, at, run):
                if at == 0:
                    ks = [k for k in range(-2, run - 1) if behind(s, least, -k, SLOT_TILES) is not None]
                    columns.update(zip(ks, weight_columns(s + ks[0], len(ks))))
                j = behind(s, least, 0, SLOT_TILES)
                if j is not None:
                    pe.wait_ge(e_in[r], 16 * (turn + 1))
                    if least:
                        pe.wait_ge(e_xT_sb, j)
                    mm(psum[:, 6, 0:P], xs[:, r, 0:DIM], ident, is_transpose=True, start=True, stop=True).then_inc(e_xT, 1)
                j = behind(s, least, 1, SLOT_TILES)
                if j is not None:
                    q = (r - 1) % RING
                    col = columns[at - 1]
                    large, small = w1_hi[:, bass.ds(col, HID)], w1_lo[:, bass.ds(col, HID)]
                    pe.wait_ge(e_x, j + 1)
                    for c in range(CHUNKS):
                        chunk = slice(c * P, (c + 1) * P)
                        into = psum[:, q, chunk]
                        mm(into, large[:, chunk], xs_hi[:, q, :], start=True, stop=False)
                        mm(into, large[:, chunk], xs_lo[:, q, :], start=False, stop=False)
                        last = mm(into, small[:, chunk], xs_hi[:, q, :], start=False, stop=True)
                    last.then_inc(e_up, 1)
                j = behind(s, least, 2, SLOT_TILES)
                if j is not None:
                    q = (r - 2) % RING
                    col = columns[at - 2]
                    pe.wait_ge(e_h, j + 1)
                    if least - 2 >= RING:
                        pe.wait_ge(e_y, j - RING + 1)
                    for c in range(CHUNKS):
                        chunk = slice(c * P, (c + 1) * P)
                        both = w2_both[:, bass.ds(2 * col + c * 2 * DIM, 2 * DIM)]
                        mm(psum[:, 3 + q, 0:2 * DIM], hs_hi[:, q, chunk], both, start=c == 0, stop=False,
                           skip_group_check=True)
                        last = mm(psum[:, 3 + q, 0:DIM], hs_lo[:, q, chunk], both[:, 0:DIM], start=False,
                                  stop=c == CHUNKS - 1, skip_group_check=True)
                    last.then_inc(e_down, 1)

            pe.wait_ge(tables, 1)
            pe.wait_ge(w_lo, 2)
            expert_pipeline(pe, expert_step, 2)


def constants(np):
    c = np.zeros((P, CONST_COLS), np.float32)

    def put(name, a):
        lo, hi = CONST[name]
        c[:, lo:hi] = a
    p = np.arange(P)
    put("ident", np.eye(P))
    put("pick", np.tile(np.eye(64), (2, 2)))
    put("head_mask", p[:, None] // HD % HALF == np.arange(HALF))
    q = np.arange(SEQ)
    dist = np.minimum(q[None, :] - q[:, None], 0) * (8.0 / SCALE)
    put("dist_qk", np.tile(dist, (2, 1)))
    inv = (1.0 / 10000.0 ** (np.arange(0, HD, 2, dtype=np.float32) / HD)).astype(np.float32)
    ang = (q.astype(np.float32)[:, None] * inv[None, :]).astype(np.float32)
    put("cos", np.cos(ang).T[p % 4])
    put("sin", np.sin(ang).T[p % 4] * np.where(p % HD < 4, -1.0, 1.0)[:, None])
    put("before", p[:, None] < p[None, :])
    put("first", np.broadcast_to(EXPERTS - np.arange(EXPERTS), (P, EXPERTS)))
    put("slot128", np.broadcast_to(P * np.arange(TILES), (P, TILES)))
    tile = np.arange(SLOT_TILES)
    put("tile_no", np.broadcast_to(tile, (P, SLOT_TILES)))
    e = np.arange(EXPERTS)
    up, region = e % 2 == 0, e // 2 * REGION
    put("slot_sign", np.broadcast_to(np.where(up, 1, -1), (P, EXPERTS)))
    put("slot_base", np.broadcast_to(np.where(up, region, region + REGION - 1), (P, EXPERTS)))
    put("tile_step", np.broadcast_to(np.where(up, P, -P), (P, EXPERTS)))
    idle = EXPERTS // 2 * REGION + P * np.maximum(tile - TILES, 0)
    base = np.where(up, region, region + REGION - P)[None, :] - idle[:, None]
    put("tile_base", np.broadcast_to(base.reshape(-1), (P, SLOT_TILES * EXPERTS)))
    put("spare", P * np.arange(RUN)[None, :] + p[:, None])
    put("token", SPARE + P * np.arange(TILES)[None, :] + p[:, None])
    put("idle_row", np.broadcast_to(idle, (P, SLOT_TILES)))
    return c


def kernel(**inputs):
    import numpy as np
    import concourse.bacc as bacc
    from concourse.bass_utils import run_bass_kernel_spmd

    a = {k: np.asarray(v) for k, v in inputs.items()}

    qkv = a["L0_attn_qkv_w"].T
    parted = np.arange(DIM).reshape(PAIRS, 2, HD).transpose(1, 0, 2).reshape(-1)
    by_parted = lambda w: w[:, parted]
    rotated = np.arange(DIM) // HD * HD + (np.arange(DIM) + HD // 2) % HD
    every = lambda v: np.broadcast_to(v, (P, v.shape[-1]))
    arrays = {
        "consts": constants(np),
        "x": a["x"], "ctx": a["ctx_1024"],
        "wqkv": np.concatenate([qkv[:, :2 * DIM], by_parted(qkv[:, 2 * DIM:]),
                                a["L0_xattn_Wq"].T, a["L0_xattn_Wk"].T, by_parted(a["L0_xattn_Wv"].T),
                                a["L0_ffn_w_qkv"][:, :2 * DIM], by_parted(a["L0_ffn_w_qkv"][:, 2 * DIM:])], 1),
        "wrot": np.concatenate([qkv[:, rotated], qkv[:, DIM + rotated]], 1),
        "wo": np.concatenate([a["L0_attn_proj_w"].T, a["L0_xattn_Wo"].T, a["L0_ffn_w_proj"]], 1),
        "bv": np.repeat(a["L0_xattn_bv"][parted].reshape(2, 1, DIM // 2), 64, 1).reshape(P, DIM // 2),
        "cols": np.stack([a["L0_xattn_bq"], a["L0_xattn_bk"], a["L0_ffn_ln1_w"], a["L0_ffn_ln1_b"],
                          a["L0_ffn_ln2_w"], a["L0_ffn_ln2_b"]], 1),
        "rows": np.concatenate([every(a[k]) for k in ("L0_attn_proj_b", "L0_xattn_bo")], 1),
        "slopes": every(a["L0_attn_slopes"]),
        "gate_w": a["L0_ffn_gate_w"], "gate_b": every(a["L0_ffn_gate_b"]),
        "w1": a["L0_ffn_w1"].transpose(1, 0, 2).reshape(P, EXPERTS * HID),
        "w2": a["L0_ffn_w2"].reshape(EXPERTS, CHUNKS, P, DIM).transpose(2, 0, 1, 3).reshape(P, EXPERTS * HID),
    }
    arrays = {k: np.ascontiguousarray(v) for k, v in arrays.items()}
    nc = bacc.Bacc("TRN2", target_bir_lowering=False, num_devices=1)
    ins = {k: nc.dram_tensor(f"in_{k}", v.shape, mybir.dt.from_np(v.dtype), kind="ExternalInput").ap()
           for k, v in arrays.items()}
    out = nc.dram_tensor("out_x", (SEQS, SEQ, DIM), F32, kind="ExternalOutput").ap()
    slots = nc.dram_tensor("slots", (SLOT_ROWS, DIM + 1), F32, kind="Internal").ap()
    results = nc.dram_tensor("results", (SPARE + TOKENS, DIM), F32, kind="Internal").ap()
    decoder(nc, ins, out, slots, results)
    r = run_bass_kernel_spmd(nc, [{f"in_{k}": v for k, v in arrays.items()}], core_ids=[0])
    return r.results[0]["out_x"]
```
